# Optimizing a Trainium2 kernel written in Bass

```python
import numpy as np
import jax
import jax.numpy as jnp

def _softmax(x, axis=-1):
    return jax.nn.softmax(x, axis=axis)

def _gelu(x):
    return jax.nn.gelu(x, approximate=True)

def _silu(x):
    return jax.nn.silu(x)

def _sigmoid(x):
    return jax.nn.sigmoid(x)

def _layernorm(x, axis=-1, eps=1e-05):
    m = jnp.mean(x, axis=axis, keepdims=True)
    v = jnp.var(x, axis=axis, keepdims=True)
    return (x - m) / jnp.sqrt(v + eps)

def _scatter_add(tgt, idx, src, axis=0):
    return tgt.at[idx].add(src)

def _segment_sum(src, seg, n):
    return jax.ops.segment_sum(src, seg, n)
kernel_name = 'mk_adj_preln_d1_adj_r2_a41190'

def setup_inputs(seed: int=0):
    np.random.seed(seed)
    _w = jnp.asarray

    def _rec_inputs():
        import jax
        import jax.numpy as jnp
        _gk = jax.random.key(seed)
        x = -0.0005146 + 1 * jax.random.normal(jax.random.fold_in(_gk, 1), (8, 1024, 128), jnp.float32)
        _a = jax.random.bernoulli(jax.random.fold_in(_gk, 2), 0.015625, (8, 1024, 1024))
        adj = _a.astype(jnp.int32)
        return (x, adj)
    x, adj = _rec_inputs()

    def _L0_gnn_setup():
        import jax, jax.numpy as jnp
        import numpy as np
        B, N, C, OUT, S = (4, 1024, 128, 128, 25)
        DENSITY = 0.008
        key = jax.random.key(seed)
        kA, kX, kW = jax.random.split(key, 3)
        A = jax.random.bernoulli(kA, DENSITY, (B, N, N)).astype(jnp.int32)
        X = jax.random.normal(kX, (B, N, C), dtype=jnp.float32)
        W = jax.random.normal(kW, (2 * C, OUT), dtype=jnp.float32) * np.float32(1.0 / np.sqrt(2 * C))
        b = jnp.zeros((OUT,), dtype=jnp.float32)
        return {'A': A, 'X': X, 'W': W, 'b': b}
    _L0_gnn_all = _L0_gnn_setup()
    _L0_gnn_in = {k: v for k, v in _L0_gnn_all.items() if k in ('W', 'b')}
    del _L0_gnn_all
    return {'x': x, 'adj': adj, 'L0_gnn_W': _L0_gnn_in['W'], 'L0_gnn_b': _L0_gnn_in['b']}

def reference(x, adj, L0_gnn_W, L0_gnn_b):
    import jax
    import jax.numpy as jnp

    def _L0_gnn_ref(A, X, W, b):
        import jax, jax.numpy as jnp
        import numpy as np
        B, N, C, OUT, S = (4, 1024, 128, 128, 25)
        DENSITY = 0.008
        mask = A != 0
        neg_inf = jnp.float32(-jnp.inf)
        pri = -jnp.arange(N, dtype=jnp.float32)
        scores = jnp.where(mask, pri, neg_inf)
        vals, idx = jax.lax.top_k(scores, S)
        valid = vals > neg_inf
        feats = jax.vmap(lambda x, i: x[i])(X, idx)
        feats = jnp.where(valid[..., None], feats, neg_inf)
        agg = feats.max(axis=2)
        degree = mask.sum(axis=-1)
        agg = jnp.where((degree <= S)[..., None], jnp.maximum(agg, 0.0), agg)
        h = jnp.concatenate([X, agg], axis=-1)
        out = jax.nn.relu(jnp.einsum('bnf,fo->bno', h, W) + b)
        return out
    h = jnp.maximum(_layernorm(x, axis=-1), 0.0)
    x = x + _L0_gnn_ref(adj, h, L0_gnn_W, L0_gnn_b)
    return x

_drawn_inputs = setup_inputs


def setup_inputs(seed=0):
    import zlib

    import numpy as np

    out = dict(_drawn_inputs(seed))
    spreads = {'L0_gnn_b': (0.0, 0.1)}
    factors = {}
    for name, (base, spread) in spreads.items():
        noise = np.random.default_rng([zlib.crc32(name.encode()), seed]).standard_normal(out[name].shape)
        drawn = base * np.exp(spread * noise) if base else spread * noise
        out[name] = jnp.asarray(drawn.astype(out[name].dtype))
    for name, factor in factors.items():
        out[name] = (out[name] * factor).astype(out[name].dtype)
    return out
```

```python
from contextlib import ExitStack

import concourse.bass as bass
from concourse import mybir

F32 = mybir.dt.float32
F16 = mybir.dt.float16
I32 = mybir.dt.int32
ALU = mybir.AluOpType
ACT = mybir.ActivationFunctionType

P = 128
LIMIT = 25
EPS = 1e-5
SCALE = 4096.0
STATIC = 8
EDGE = 1050
MARK = 512
CODE_AT = MARK // 2
LOOKAHEAD = 3
ONEHOTS = 4
WIDTH = 512


def adj_preln_kernel(nc, x, xT, adjT, W, b, outT):
    B, N, C = x.shape
    K = N // P
    H = N // WIDTH
    PREP = H * K
    SLOTS = K * STATIC
    SPREAD = SLOTS // PREP

    ctx = ExitStack()
    with ctx:
        def sb(name, shape, dt):
            return ctx.enter_context(nc.sbuf_tensor(name, shape, dt))

        def sem(name):
            return ctx.enter_context(nc.semaphore(name))

        adj_in = sb("adj_in", [P, K, N], I32)
        nonedge = sb("nonedge", [P, K, N], F16)
        valid = sb("valid", [P, 2, WIDTH], F16)
        code = sb("code", [P, 2, K, N], F16)
        onehot = sb("onehot", [P, ONEHOTS, N], F16)
        tail_onehot = sb("tail_onehot", [P, N], F16)
        x_in = sb("x_in", [P, K, C], F32)
        stats = sb("stats", [P, K, 6], F32)
        mv = sb("mv", [P, K, 2], F32)
        var_eps = sb("var_eps", [P, K], F32)
        rstd = sb("rstd", [P, K], F32)
        rstd_s = sb("rstd_s", [P, K], F32)
        mean_neg = sb("mean_neg", [P, K], F32)
        shift = sb("shift", [P, K], F32)
        h32 = sb("h32", [P, K, C], F32)
        h16 = sb("h16", [P, 2, 2, K, C], F16)
        hT = sb("hT", [P, N], F32)
        agg = sb("agg", [P, N], F32)
        xT_in = sb("xT_in", [P, N], F32)
        act_out = sb("act_out", [P, N], F32)
        out_sb = sb("out_sb", [P, N], F32)
        over = sb("over", [P, 2], F32)
        over_sum = sb("over_sum", [P, 1], F32)
        over_int = sb("over_int", [P, 1], I32)
        over_junk = sb("over_junk", [P, WIDTH], F16)
        tail_last = sb("tail_last", [1, 2, K], I32)
        w_in = sb("w_in", [P, 2, C], F32)
        w_sb = sb("w_sb", [P, 2, C], F32)
        b_sb = sb("b_sb", [P, 1], F32)
        count_here = sb("count_here", [P, P], F16)
        count_rest = sb("count_rest", [P, P], F16)
        number = sb("number", [P, P], F16)
        ident = sb("ident", [P, P], F16)
        pick_row = sb("pick_row", [P, K, P], F16)
        iota_i = sb("iota_i", [P, K], I32)
        iota_s = sb("iota_s", [P, LIMIT + 1], I32)
        iota_f = sb("iota_f", [P, K], F32)
        valid_bias = sb("valid_bias", [P, K], F32)
        code_bias = sb("code_bias", [P, 1], F32)
        over_bias = sb("over_bias", [P, 1], F32)
        slot_code = sb("slot_code", [P, LIMIT + 1], F32)
        minus_half = sb("minus_half", [P, K], F32)

        gathered = [ctx.enter_context(nc.psum_tensor(f"gathered{i}", [P, N], F32)) for i in range(2)]
        ordinal_ps = ctx.enter_context(nc.psum_tensor("ordinal_ps", [P, WIDTH], F32))
        number_ps = ctx.enter_context(nc.psum_tensor("number_ps", [P, WIDTH], F32))
        degree_ps = ctx.enter_context(nc.psum_tensor("degree_ps", [P, WIDTH], F32))
        dense_ps = ctx.enter_context(nc.psum_tensor("dense_ps", [P, WIDTH], F32))

        adj_loaded = [sem(f"adj_loaded{k}") for k in range(K)]
        x_loaded = sem("x_loaded")
        xT_loaded = sem("xT_loaded")
        w_loaded = sem("w_loaded")
        const_set = sem("const_set")
        const_ready = sem("const_ready")
        bias_ready = sem("bias_ready")
        w_ready = sem("w_ready")
        nonedge_ready = sem("nonedge_ready")
        ordinal_ready = sem("ordinal_ready")
        valid_ready = sem("valid_ready")
        number_ready = sem("number_ready")
        code_ready = sem("code_ready")
        over_ready = sem("over_ready")
        over_summed = sem("over_summed")
        over_converted = sem("over_converted")
        tail_loaded = sem("tail_loaded")
        onehot_ready = sem("onehot_ready")
        gather_ready = sem("gather_ready")
        max_done = sem("max_done")
        tail_onehot_ready = sem("tail_onehot_ready")
        tail_gather_ready = sem("tail_gather_ready")
        tail_max_done = sem("tail_max_done")
        agg_done = sem("agg_done")
        stats_part = sem("stats_part")
        stats_ready = sem("stats_ready")
        pool_step = sem("pool_step")
        norm_ready = sem("norm_ready")
        h32_ready = sem("h32_ready")
        hi_ready = sem("hi_ready")
        lo_ready = sem("lo_ready")
        dense_ready = sem("dense_ready")
        dense_read = sem("dense_read")
        added = sem("added")
        stored = sem("stored")

        passed = {name: sem(f"{name}_passed") for name in ("pool", "dve", "pe")}

        def hold(eng, name, semaphore, value):
            eng.wait_ge(semaphore, value)
            eng.sem_inc(passed[name], 1)

        block = ctx.enter_context(nc.Block())

        @block.sync
        def _(sp):
            for part in range(2):
                sp.dma_start(w_in[:, part, :], W[part * C:(part + 1) * C, :]).then_inc(w_loaded, 16)
            sp.dma_start(b_sb[:, :], b.rearrange("(o u) -> o u", u=1)).then_inc(w_loaded, 16)

            def load(nb, first):
                if not first:
                    sp.wait_ge(hi_ready, nb)
                    sp.wait_ge(stats_ready, nb)
                sp.dma_start(x_in[:, :, :], x[nb].rearrange("(k p) c -> p k c", p=P)).then_inc(x_loaded, 16)
                for k in range(K):
                    if not first:
                        sp.wait_ge(nonedge_ready, K * (nb - 1) + k + 1)
                    sp.dma_start(adj_in[:, k, :], adjT[nb, k * P:(k + 1) * P, :]).then_inc(adj_loaded[k], 16)

            def load_xT(nb, first):
                if not first:
                    sp.wait_ge(added, nb + 1)
                sp.dma_start(xT_in[:, :], xT[nb]).then_inc(xT_loaded, 16)

            load(0, True)
            load_xT(0, True)
            load(1, False)
            with sp.Fori(2, B) as nb:
                load(nb, False)
                load_xT(nb - 1, False)
            load_xT(B - 1, False)

        @block.gpsimd
        def _(pool):
            pool.sem_inc(added, 1)
            n_set = 0
            for t, v in ((count_here, 1.0), (count_rest, 1.0), (number, 1.0), (ident, 0.0), (pick_row, 0.0),
                         (minus_half, -0.5), (over_bias, P / 2 - STATIC)):
                pool.memset(t[:] if len(t.shape) == 2 else t[:, :, :], v).then_inc(const_set, 1)
                n_set += 1
            pool.iota(iota_i[:, :], [[P, K]], base=0, channel_multiplier=1).then_inc(const_set, 1)
            pool.iota(iota_s[:, :], [[1, LIMIT + 1]], base=0, channel_multiplier=0).then_inc(const_set, 1)
            n_set += 2
            pool.wait_ge(const_set, n_set)
            for t, sign, base in ((count_here, 1, 0), (number, 1, 0), (count_rest, -1, -1)):
                pool.affine_select(out=t[:, :], in_=t[:, :], compare_op=ALU.is_ge, fill=0.0, base=base,
                                   pattern=[[sign, P]], channel_multiplier=-sign).then_inc(const_set, 1)
            pool.tensor_copy(iota_f[:, :], iota_i[:, :]).then_inc(const_set, 1)
            pool.tensor_copy(slot_code[:, :], iota_s[:, :]).then_inc(const_set, 1)
            n_set += 5
            pool.wait_ge(const_set, n_set)
            for t, diagonal in ((count_here, 1.0 - EDGE), (count_rest, float(EDGE)), (number, 1.0 + MARK),
                                (ident, 1.0)):
                pool.affine_select(out=t[:, :], in_=t[:, :], compare_op=ALU.not_equal, fill=diagonal, base=0,
                                   pattern=[[-1, P]], channel_multiplier=1).then_inc(const_ready, 1)
            for k in range(K):
                pool.memset(pick_row[:, k, k:k + 1], 1.0).then_inc(const_ready, 1)
            pool.tensor_scalar(valid_bias[:, :], iota_f[:, :], -1.0, LIMIT - 0.5, ALU.mult, ALU.add).then_inc(bias_ready, 1)
            pool.tensor_scalar(code_bias[:, :], iota_f[:, 0:1], 0.5, 0.5, ALU.mult, ALU.add).then_inc(bias_ready, 1)

            def nonedges(nb, ks):
                for k in ks:
                    hold(pool, "pool", adj_loaded[k], 16 * (nb + 1))
                    if not (isinstance(nb, int) and nb == 0):
                        hold(pool, "pool", ordinal_ready, PREP * (nb - 1) + min(PREP, (H - 1) * K + k + 2))
                    pool.tensor_scalar(nonedge[:, k, :], adj_in[:, k, :], 0.0, None, ALU.is_equal).then_inc(nonedge_ready, 1)

            def norm(nb):
                hold(pool, "pool", stats_ready, nb + 1)
                if not (isinstance(nb, int) and nb == 0):
                    hold(pool, "pool", h32_ready, nb)
                pool.tensor_scalar(var_eps[:, :], mv[:, :, 1], EPS, None, ALU.add).then_inc(pool_step, 1)
                pool.tensor_scalar(mean_neg[:, :], mv[:, :, 0], -1.0, None, ALU.mult).then_inc(pool_step, 1)
                hold(pool, "pool", pool_step, 4 * nb + 2)
                pool.tensor_tensor(rstd[:, :], var_eps[:, :], minus_half[:, :], ALU.pow).then_inc(pool_step, 1)
                hold(pool, "pool", pool_step, 4 * nb + 3)
                pool.tensor_scalar(rstd_s[:, :], rstd[:, :], SCALE, None, ALU.mult).then_inc(pool_step, 1)
                hold(pool, "pool", pool_step, 4 * nb + 4)
                pool.tensor_tensor(shift[:, :], mean_neg[:, :], rstd_s[:, :], ALU.mult).then_inc(norm_ready, 1)

            def low_part(nb, par):
                pool.wait_ge(hi_ready, nb + 1)
                pool.tensor_tensor(h16[:, par, 1, :, :], h32[:, :, :], h16[:, par, 0, :, :], ALU.subtract).then_inc(lo_ready, 1)

            def tail_counts(nb, par):
                hold(pool, "pool", over_ready, H * (nb + 1))
                pool.tensor_tensor(over_sum[0:K, :], over[0:K, 0:1], over[0:K, 1:2], ALU.add).then_inc(over_summed, 1)
                hold(pool, "pool", over_summed, nb + 1)
                if not (isinstance(nb, int) and nb == 0):
                    hold(pool, "pool", tail_loaded, 16 * nb)
                pool.tensor_copy(over_int[0:K, :], over_sum[0:K, :]).then_inc(over_converted, 1)
                hold(pool, "pool", over_converted, nb + 1)
                pool.dma_start(tail_last[0:1, par, :], over_int[0:K, :]).then_inc(tail_loaded, 16)

            def finish(b):
                pool.wait_ge(dense_read, 4 * b + 5)
                pool.wait_ge(xT_loaded, 16 * (b + 1))
                if not (isinstance(b, int) and b == 0):
                    pool.wait_ge(stored, 16 * b)
                pool.tensor_tensor(out_sb[:, :], act_out[:, :], xT_in[:, :], ALU.add).then_inc(added, 1)
                pool.wait_ge(added, b + 2)
                pool.dma_start(outT[b], out_sb[:, :]).then_inc(stored, 16)

            nonedges(0, range(K))
            norm(0)
            low_part(0, 0)
            tail_counts(0, 0)
            nonedges(1, range(K // 2))
            with pool.Fori(1, B - 1) as nb:
                par = nb & 1
                nonedges(nb, range(K // 2, K))
                norm(nb)
                low_part(nb, par)
                nonedges(nb + 1, range(K // 2))
                tail_counts(nb, par)
                finish(nb - 1)
            nonedges(B - 1, range(K // 2, K))
            norm(B - 1)
            low_part(B - 1, (B - 1) & 1)
            tail_counts(B - 1, (B - 1) & 1)
            finish(B - 2)
            finish(B - 1)
            pool.wait_ge(stored, 16 * B)

        @block.scalar
        def _(act):
            act.sem_inc(dense_read, 1)
            act.wait_ge(bias_ready, 2)
            act.wait_ge(const_set, 7)

            def edges(nb, p):
                half, k = divmod(p, K)
                act.wait_ge(ordinal_ready, PREP * nb + p + 1)
                if not (isinstance(nb, int) and nb == 0 and p < 2):
                    act.wait_ge(number_ready, PREP * nb + p - 1)
                act.activation(valid[:, p % 2, :], ordinal_ps[:, :], ACT.Sign,
                               bias=valid_bias[:, k:k + 1]).then_inc(valid_ready, 1)

            def codes(nb, par, p):
                half, k = divmod(p, K)
                act.wait_ge(number_ready, PREP * nb + p + 1)
                if p == 0 and not (isinstance(nb, int) and nb < 2):
                    act.wait_ge(agg_done, nb - 1)
                act.activation(code[:, par, k, half * WIDTH:(half + 1) * WIDTH], number_ps[:, :], ACT.Identity,
                               bias=code_bias[:, :], scale=0.5).then_inc(code_ready, 1)
                if k == K - 1:
                    if not (isinstance(nb, int) and nb == 0):
                        act.wait_ge(over_summed, nb)
                    if half:
                        act.wait_ge(over_ready, H * nb + half)
                    act.activation(over_junk[0:K, :], degree_ps[0:K, :], ACT.Relu, bias=over_bias[0:K, :], scale=0.5,
                                   accum_out=over[0:K, half:half + 1]).then_inc(over_ready, 1)

            def make_h(nb, par):
                act.wait_ge(x_loaded, 16 * (nb + 1))
                act.wait_ge(norm_ready, nb + 1)
                if not (isinstance(nb, int) and nb == 0):
                    act.wait_ge(lo_ready, nb)
                for k in range(K):
                    last = act.activation(h32[:, k, :], x_in[:, k, :], ACT.Relu, bias=shift[:, k:k + 1],
                                          scale=rstd_s[:, k:k + 1])
                last.then_inc(h32_ready, 1)
                act.wait_ge(h32_ready, nb + 1)
                act.activation(h16[:, par, 0, :, :], h32[:, :, :], ACT.Copy).then_inc(hi_ready, 1)

            def copy_hT(b, half):
                act.wait_ge(dense_ready, 4 * b + half + 1)
                act.activation(hT[:, half * WIDTH:(half + 1) * WIDTH], dense_ps[:, :], ACT.Copy).then_inc(dense_read, 1)

            def relu_out(b, half):
                act.wait_ge(dense_ready, 4 * b + 3 + half)
                if half == 0:
                    act.wait_ge(added, b + 1)
                act.activation(act_out[:, half * WIDTH:(half + 1) * WIDTH], dense_ps[:, :], ACT.Relu,
                               bias=b_sb[:, :]).then_inc(dense_read, 1)

            def body(b, par_next, last):
                for p in range(PREP):
                    if not last:
                        edges(b + 1, p)
                        codes(b + 1, par_next, p)
                    if p == 3 or p == 5:
                        copy_hT(b, (p - 3) // 2)
                    if p == 11 and not last:
                        make_h(b + 1, par_next)
                for half in range(H):
                    relu_out(b, half)

            for p in range(PREP):
                edges(0, p)
                codes(0, 0, p)
            make_h(0, 0)
            act.wait_ge(w_loaded, 48)
            with act.Fori(0, B - 1) as b:
                body(b, (b + 1) & 1, False)
            body(B - 1, 0, True)

        @block.vector
        def _(dve):
            dve.wait_ge(w_loaded, 48)
            dve.tensor_scalar(w_sb[:, :, :], w_in[:, :, :], 1.0 / SCALE, None, ALU.mult).then_inc(w_ready, 1)

            def stats_of(nb, k):
                if k == 0:
                    dve.wait_ge(x_loaded, 16 * (nb + 1))
                dve.bn_stats(stats[:, k, :], x_in[:, k, :]).then_inc(stats_part, 1)

            def means_of(nb, k):
                if k == 0:
                    hold(dve, "dve", stats_part, K * (nb + 1))
                    if not (isinstance(nb, int) and nb == 0):
                        hold(dve, "dve", norm_ready, nb)
                last = dve.bn_aggr(mv[:, k, :], stats[:, k, :])
                if k == K - 1:
                    last.then_inc(stats_ready, 1)

            def make_onehot(b, par, n):
                k, s = n // STATIC, n % STATIC + 1
                if n == 0:
                    dve.wait_ge(code_ready, PREP * (b + 1))
                if n > LOOKAHEAD or (n < LOOKAHEAD and not (isinstance(b, int) and b == 0)):
                    dve.wait_ge(gather_ready, SLOTS * b + n + 1 - ONEHOTS)
                dve.tensor_scalar(onehot[:, n % ONEHOTS, :], code[:, par, k, :], float(CODE_AT + s), None,
                                  ALU.is_equal).then_inc(onehot_ready, 1)

            def take_max(b, n):
                dve.wait_ge(gather_ready, SLOTS * b + n + 1)
                if n == 0:
                    dve.tensor_scalar(agg[:, :], gathered[0][:, :], 0.0, None, ALU.max).then_inc(max_done, 1)
                else:
                    dve.wait_ge(max_done, SLOTS * b + n)
                    dve.tensor_tensor(agg[:, :], gathered[n % 2][:, :], agg[:, :], ALU.max).then_inc(max_done, 1)

            def tail(b, par, done):
                hold(dve, "dve", tail_loaded, 16 * (b + 1))
                for k in range(K):
                    over_k = dve.value_load(tail_last[0:1, par, k:k + 1], min_val=0, max_val=N)
                    with dve.If(over_k > 0):
                        with dve.Fori(STATIC + 1, LIMIT + 1) as s:
                            with dve.If(over_k + STATIC + 1 > s):
                                dve.reg_add(done, done, 1)
                                d = dve.snap(done)
                                dve.tensor_scalar(tail_onehot[:, :], code[:, par, k, :], float(CODE_AT),
                                                  slot_code[:, bass.ds(s, 1)], ALU.subtract,
                                                  ALU.is_equal).then_inc(tail_onehot_ready, 1)
                                dve.wait_ge(tail_gather_ready, d)
                                dve.wait_ge(max_done, SLOTS * (b + 1))
                                dve.tensor_tensor(agg[:, :], gathered[0][:, :], agg[:, :], ALU.max).then_inc(tail_max_done, 1)
                                hold(dve, "dve", tail_max_done, d)

            def body(b, par, par_next, last, done):
                for n in range(SLOTS):
                    ahead = n + LOOKAHEAD
                    if ahead < SLOTS:
                        make_onehot(b, par, ahead)
                    elif not last:
                        make_onehot(b + 1, par_next, ahead - SLOTS)
                    take_max(b, n)
                    if not last and 2 * K <= n < 3 * K:
                        stats_of(b + 1, n - 2 * K)
                    if not last and 3 * K <= n < 4 * K:
                        means_of(b + 1, n - 3 * K)
                tail(b, par, done)
                dve.wait_ge(max_done, SLOTS * (b + 1))
                dve.sem_inc(agg_done, 1)

            for k in range(K):
                stats_of(0, k)
            for k in range(K):
                means_of(0, k)
            dve.wait_ge(const_set, 14)
            for n in range(LOOKAHEAD):
                make_onehot(0, 0, n)
            done = dve.alloc_register("tail_slots_done")
            dve.reg_mov(done, 0)
            with dve.Fori(0, B - 1) as b:
                body(b, b & 1, (b + 1) & 1, False, done)
            body(B - 1, (B - 1) & 1, 0, True, done)

        @block.tensor
        def _(pe):
            pe.wait_ge(const_ready, 4 + K)

            def order(nb, p):
                half, k = divmod(p, K)
                cols = slice(half * WIDTH, (half + 1) * WIDTH)
                pe.wait_ge(nonedge_ready, K * nb + k + 1)
                if not (isinstance(nb, int) and nb == 0 and p == 0):
                    pe.wait_ge(valid_ready, PREP * nb + p)
                if k:
                    pe.matmul(ordinal_ps[:, :], count_rest[:, :], nonedge[:, k - 1, cols], start=False, stop=False,
                              skip_group_check=True)
                pe.matmul(ordinal_ps[:, :], count_here[:, :], nonedge[:, k, cols], start=(k == 0), stop=True,
                          skip_group_check=True).then_inc(ordinal_ready, 1)

            def renumber(nb, p):
                half, k = divmod(p, K)
                pe.wait_ge(valid_ready, PREP * nb + p + 1)
                if not (isinstance(nb, int) and nb == 0 and p == 0):
                    pe.wait_ge(code_ready, PREP * nb + p)
                if k == 0 and not (isinstance(nb, int) and nb == 0 and half == 0):
                    pe.wait_ge(over_ready, H * nb + half)
                pe.matmul(degree_ps[:, :], pick_row[:, k, :], valid[:, p % 2, :], start=(k == 0), stop=(k == K - 1),
                          skip_group_check=True)
                pe.matmul(number_ps[:, :], number[:, :], valid[:, p % 2, :], start=True,
                          stop=True).then_inc(number_ready, 1)

            def products(buf, par, k, hot):
                for part in range(2):
                    for half in range(H):
                        cols = slice(half * WIDTH, (half + 1) * WIDTH)
                        last = pe.matmul(buf[:, cols], h16[:, par, part, k, :], hot[:, cols], start=(part == 0),
                                         stop=(part == 1))
                return last

            def gather(b, par, n):
                pe.wait_ge(onehot_ready, SLOTS * b + n + 1)
                if n > 1:
                    pe.wait_ge(max_done, SLOTS * b + n - 1)
                products(gathered[n % 2], par, n // STATIC, onehot[:, n % ONEHOTS, :]).then_inc(gather_ready, 1)

            def transpose_h(b, par, half):
                pe.wait_ge(dense_read, 4 * b + half + 1)
                chunks = WIDTH // P
                for q in range(chunks):
                    for part in range(2):
                        last = pe.matmul(dense_ps[:, q * P:(q + 1) * P], h16[:, par, part, half * chunks + q, :],
                                         ident[:, :], start=(part == 0), stop=(part == 1))
                last.then_inc(dense_ready, 1)

            def dense(b, half):
                cols = slice(half * WIDTH, (half + 1) * WIDTH)
                if half == 0:
                    pe.wait_ge(agg_done, b + 1)
                pe.wait_ge(dense_read, 4 * b + 3 + half)
                pe.matmul(dense_ps[:, :], w_sb[:, 0, :], hT[:, cols], start=True, stop=False)
                pe.matmul(dense_ps[:, :], w_sb[:, 1, :], agg[:, cols], start=False, stop=True).then_inc(dense_ready, 1)

            def tail(b, par, done):
                hold(pe, "pe", tail_loaded, 16 * (b + 1))
                for k in range(K):
                    over_k = pe.value_load(tail_last[0:1, par, k:k + 1], min_val=0, max_val=N)
                    with pe.If(over_k > 0):
                        hold(pe, "pe", max_done, SLOTS * (b + 1))
                        with pe.Fori(STATIC + 1, LIMIT + 1) as s:
                            with pe.If(over_k + STATIC + 1 > s):
                                pe.reg_add(done, done, 1)
                                d = pe.snap(done)
                                pe.wait_ge(tail_onehot_ready, d)
                                products(gathered[0], par, k, tail_onehot).then_inc(tail_gather_ready, 1)
                                hold(pe, "pe", tail_max_done, d)

            def body(b, par, last, done):
                pe.wait_ge(lo_ready, b + 1)
                for n in range(SLOTS):
                    gather(b, par, n)
                    if not last:
                        if n % SPREAD == 0:
                            order(b + 1, n // SPREAD)
                        if n % SPREAD == SPREAD // 2:
                            renumber(b + 1, n // SPREAD)
                    if n == 12 or n == 20:
                        transpose_h(b, par, (n - 12) // 8)
                tail(b, par, done)
                for half in range(H):
                    dense(b, half)

            for p in range(PREP):
                order(0, p)
                renumber(0, p)
            pe.wait_ge(w_ready, 1)
            done = pe.alloc_register("tail_slots_done")
            pe.reg_mov(done, 0)
            with pe.Fori(0, B - 1) as b:
                body(b, b & 1, False, done)
            body(B - 1, (B - 1) & 1, True, done)


def kernel(x, adj, L0_gnn_W, L0_gnn_b):
    import numpy as np
    import concourse.bacc as bacc
    from concourse.bass_utils import run_bass_kernel_spmd

    x = np.asarray(x)
    arrays = {
        "x": np.ascontiguousarray(x),
        "x_by_channel": np.ascontiguousarray(x.transpose(0, 2, 1)),
        "adj_by_source": np.ascontiguousarray(np.asarray(adj).transpose(0, 2, 1)),
        "W": np.ascontiguousarray(L0_gnn_W),
        "b": np.ascontiguousarray(L0_gnn_b),
    }
    nc = bacc.Bacc("TRN2", target_bir_lowering=False, num_devices=1)
    args = [nc.dram_tensor(name, a.shape, mybir.dt.from_np(a.dtype), kind="ExternalInput").ap()
            for name, a in arrays.items()]
    B, N, C = x.shape
    out = nc.dram_tensor("out_by_channel", (B, C, N), F32, kind="ExternalOutput").ap()
    adj_preln_kernel(nc, *args, out)
    r = run_bass_kernel_spmd(nc, [arrays], core_ids=[0])
    return np.ascontiguousarray(r.results[0]["out_by_channel"].transpose(0, 2, 1))
```

```python
from contextlib import ExitStack

import concourse.bass as bass
from concourse import mybir

F32 = mybir.dt.float32
F16 = mybir.dt.float16
I32 = mybir.dt.int32
ALU = mybir.AluOpType
ACT = mybir.ActivationFunctionType

P = 128
LIMIT = 25
EPS = 1e-5
SCALE = 4096.0
STATIC = 8
EDGE = 1050
MARK = 512
CODE_AT = MARK // 2
PAIR = 13
SHARED = 2 * STATIC - PAIR
FROM_ACT = (4, 5, 10, 12)
AHEAD_ACT = 2
LOOKAHEAD = 3
ONEHOTS = 8
WIDTH = 512


def adj_preln_kernel(nc, x, xT, adjT, W, b, outT):
    B, N, C = x.shape
    K = N // P
    H = N // WIDTH
    PREP = H * K
    PAIRS = K // 2
    SLOTS = PAIRS * PAIR
    STEPS = PREP // PAIRS
    ORDER_AT = (1, 4, 9, 12)
    RENUMBER_AT = (2, 5, 10, 13)
    assert len(FROM_ACT) == len(ORDER_AT) == len(RENUMBER_AT) == STEPS

    def parts(t):
        return [(c, s) for c, s in ((0, t), (1, PAIR + 1 - t)) if s <= STATIC]

    BY_DVE = [(t, q) for t in range(1, PAIR + 1) if t not in FROM_ACT for q in range(len(parts(t)))]
    assert PAIRS * len(BY_DVE) % ONEHOTS == 0

    def onehot_index(pair, t, q):
        return pair * len(BY_DVE) + BY_DVE.index((t, q))

    ctx = ExitStack()
    with ctx:
        def sb(name, shape, dt):
            return ctx.enter_context(nc.sbuf_tensor(name, shape, dt))

        def sem(name):
            return ctx.enter_context(nc.semaphore(name))

        adj_in = sb("adj_in", [P, K, N], I32)
        nonedge = sb("nonedge", [P, K, N], F16)
        valid = sb("valid", [P, 2, WIDTH], F16)
        code = sb("code", [P, 2, K, N], F16)
        onehot = sb("onehot", [P, ONEHOTS, N], F16)
        tail_onehot = sb("tail_onehot", [P, N], F16)
        x_in = sb("x_in", [P, K, C], F32)
        stats = sb("stats", [P, K, 6], F32)
        mv = sb("mv", [P, K, 2], F32)
        var_eps = sb("var_eps", [P, K], F32)
        rstd = sb("rstd", [P, K], F32)
        rstd_s = sb("rstd_s", [P, K], F32)
        mean_neg = sb("mean_neg", [P, K], F32)
        shift = sb("shift", [P, K], F32)
        h32 = sb("h32", [P, K, C], F32)
        h16 = sb("h16", [P, 2, 2, K, C], F16)
        hT = sb("hT", [P, N], F32)
        agg = sb("agg", [P, 2, N], F32)
        act_onehot = sb("act_onehot", [P, STEPS, N], F16)
        distance = sb("distance", [P, N], F16)
        xT_in = sb("xT_in", [P, N], F32)
        act_out = sb("act_out", [P, N], F32)
        out_sb = sb("out_sb", [P, N], F32)
        over = sb("over", [P, 2], F32)
        over_sum = sb("over_sum", [P, 1], F32)
        tail_f = sb("tail_f", [1, K + 2 * PAIRS], F32)
        tail_clip = sb("tail_clip", [1, K + 2 * PAIRS], F32)
        over_junk = sb("over_junk", [P, WIDTH], F16)
        tail_word = sb("tail_word", [1, 2, K + 2 * PAIRS], I32)
        w_in = sb("w_in", [P, 2, C], F32)
        w_sb = sb("w_sb", [P, 2, C], F32)
        b_sb = sb("b_sb", [P, 1], F32)
        count_here = sb("count_here", [P, P], F16)
        count_rest = sb("count_rest", [P, P], F16)
        number = sb("number", [P, P], F16)
        ident = sb("ident", [P, P], F16)
        pick_row = sb("pick_row", [P, K, P], F16)
        iota_i = sb("iota_i", [P, K], I32)
        iota_s = sb("iota_s", [P, LIMIT + 1], I32)
        iota_f = sb("iota_f", [P, K], F32)
        valid_bias = sb("valid_bias", [P, K], F32)
        code_bias = sb("code_bias", [P, 1], F32)
        over_bias = sb("over_bias", [P, 1], F32)
        slot_code = sb("slot_code", [P, LIMIT + 1], F32)
        act_target = sb("act_target", [P, LIMIT + 1], F32)
        minus_half = sb("minus_half", [P, K], F32)

        gathered = [ctx.enter_context(nc.psum_tensor(f"gathered{i}", [P, N], F32)) for i in range(2)]
        ordinal_ps = ctx.enter_context(nc.psum_tensor("ordinal_ps", [P, WIDTH], F32))
        number_ps = ctx.enter_context(nc.psum_tensor("number_ps", [P, WIDTH], F32))
        degree_ps = ctx.enter_context(nc.psum_tensor("degree_ps", [P, WIDTH], F32))
        dense_ps = ctx.enter_context(nc.psum_tensor("dense_ps", [P, WIDTH], F32))

        adj_loaded = [sem(f"adj_loaded{k}") for k in range(K)]
        x_loaded = sem("x_loaded")
        xT_loaded = sem("xT_loaded")
        w_loaded = sem("w_loaded")
        const_set = sem("const_set")
        const_ready = sem("const_ready")
        bias_ready = sem("bias_ready")
        w_ready = sem("w_ready")
        nonedge_ready = sem("nonedge_ready")
        ordinal_ready = sem("ordinal_ready")
        valid_ready = sem("valid_ready")
        number_ready = sem("number_ready")
        code_ready = sem("code_ready")
        over_ready = sem("over_ready")
        over_summed = sem("over_summed")
        tail_row = sem("tail_row")
        tail_any = sem("tail_any")
        distance_ready = sem("distance_ready")
        act_onehot_ready = sem("act_onehot_ready")
        last_added = sem("last_added")
        last_stored = sem("last_stored")
        tail_loaded = sem("tail_loaded")
        onehot_ready = sem("onehot_ready")
        gather_ready = sem("gather_ready")
        max_done = sem("max_done")
        tail_onehot_ready = sem("tail_onehot_ready")
        tail_gather_ready = sem("tail_gather_ready")
        tail_max_done = sem("tail_max_done")
        agg_done = sem("agg_done")
        stats_part = sem("stats_part")
        stats_ready = sem("stats_ready")
        pool_step = sem("pool_step")
        norm_ready = sem("norm_ready")
        h32_ready = sem("h32_ready")
        hi_ready = sem("hi_ready")
        lo_ready = sem("lo_ready")
        dense_ready = sem("dense_ready")
        dense_read = sem("dense_read")
        added = sem("added")
        stored = sem("stored")

        passed = {name: sem(f"{name}_passed") for name in ("pool", "dve", "pe", "act")}

        def hold(eng, name, semaphore, value):
            eng.wait_ge(semaphore, value)
            eng.sem_inc(passed[name], 1)

        def tail(eng, name, b, par, pair, done, tail_slot):
            n_next = PAIR * (pair + 1)
            if pair == 0:
                hold(eng, name, tail_loaded, b + 1)

            def word(i):
                return eng.value_load(tail_word[0:1, par, i:i + 1], min_val=0, max_val=LIMIT - STATIC)

            with eng.If(word(K + PAIRS + pair) > 0):
                with eng.If(word(K + pair) > 0):
                    with eng.Fori(PAIR + 1 - STATIC, STATIC + 1) as s:
                        tail_slot(b, par, 2 * pair + 1, n_next, s, done)
                    eng.sem_inc(passed[name], 1)
                for k in (2 * pair, 2 * pair + 1):
                    over_k = word(k)
                    with eng.If(over_k > 0):
                        with eng.Fori(STATIC + 1, over_k + STATIC + 1) as s:
                            tail_slot(b, par, k, n_next, s, done)
                        eng.sem_inc(passed[name], 1)
                eng.sem_inc(passed[name], 1)

        block = ctx.enter_context(nc.Block())

        @block.sync
        def _(sp):
            def load(nb, first):
                if not first:
                    sp.wait_ge(hi_ready, nb)
                    sp.wait_ge(stats_ready, nb)
                sp.dma_start(x_in[:, :, :], x[nb].rearrange("(k p) c -> p k c", p=P)).then_inc(x_loaded, 16)
                for k in range(K):
                    if not first:
                        sp.wait_ge(nonedge_ready, K * (nb - 1) + k + 1)
                    sp.dma_start(adj_in[:, k, :], adjT[nb, k * P:(k + 1) * P, :]).then_inc(adj_loaded[k], 16)

            def load_xT(nb, first):
                if not first:
                    sp.wait_ge(added, nb + 1)
                sp.dma_start(xT_in[:, :], xT[nb]).then_inc(xT_loaded, 16)

            load(0, True)
            for part in range(2):
                sp.dma_start(w_in[:, part, :], W[part * C:(part + 1) * C, :]).then_inc(w_loaded, 16)
            sp.dma_start(b_sb[:, :], b.rearrange("(o u) -> o u", u=1)).then_inc(w_loaded, 16)
            load_xT(0, True)
            load(1, False)
            with sp.Fori(2, B) as nb:
                load(nb, False)
                load_xT(nb - 1, False)
            load_xT(B - 1, False)
            for half in range(H):
                cols = slice(half * WIDTH, (half + 1) * WIDTH)
                sp.wait_ge(last_added, half + 1)
                sp.dma_start(outT[B - 1, :, cols], out_sb[:, cols]).then_inc(last_stored, 16)
            sp.wait_ge(stored, 16 * (B - 1))
            sp.wait_ge(last_stored, 16 * H)

        @block.gpsimd
        def _(pool):
            pool.sem_inc(added, 1)
            n_set = 0
            for t, v in ((count_here, 1.0), (count_rest, 1.0), (number, 1.0), (ident, 0.0), (pick_row, 0.0),
                         (minus_half, -0.5), (over_bias, float(P - PAIR))):
                pool.memset(t[:, :] if len(t.shape) == 2 else t[:, :, :], v).then_inc(const_set, 1)
                n_set += 1
            pool.iota(iota_i[:, :], [[P, K]], base=0, channel_multiplier=1).then_inc(const_set, 1)
            pool.iota(iota_s[:, :], [[1, LIMIT + 1]], base=0, channel_multiplier=0).then_inc(const_set, 1)
            n_set += 2
            pool.wait_ge(const_set, n_set)
            for t, sign, base in ((count_here, 1, 0), (number, 1, 0), (count_rest, -1, -1)):
                pool.affine_select(out=t[:, :], in_=t[:, :], compare_op=ALU.is_ge, fill=0.0, base=base,
                                   pattern=[[sign, P]], channel_multiplier=-sign).then_inc(const_set, 1)
            pool.tensor_copy(iota_f[:, :], iota_i[:, :]).then_inc(const_set, 1)
            pool.tensor_copy(slot_code[:, :], iota_s[:, :]).then_inc(const_set, 1)
            n_set += 5
            pool.wait_ge(const_set, n_set)
            for t, diagonal in ((count_here, 1.0 - EDGE), (count_rest, float(EDGE)), (number, 1.0 + MARK),
                                (ident, 1.0)):
                pool.affine_select(out=t[:, :], in_=t[:, :], compare_op=ALU.not_equal, fill=diagonal, base=0,
                                   pattern=[[-1, P]], channel_multiplier=1).then_inc(const_ready, 1)
            for k in range(K):
                pool.memset(pick_row[:, k, k:k + 1], 1.0).then_inc(const_ready, 1)
                pool.memset(pick_row[:, k, K + k // 2:K + k // 2 + 1], 1.0).then_inc(const_ready, 1)
            pool.memset(over_bias[0:K, :], P / 2 - STATIC).then_inc(const_ready, 1)
            pool.tensor_scalar(valid_bias[:, :], iota_f[:, :], -1.0, LIMIT - 0.5, ALU.mult, ALU.add).then_inc(bias_ready, 1)
            pool.tensor_scalar(act_target[:, :], slot_code[:, :], -1.0, -float(CODE_AT), ALU.mult, ALU.add).then_inc(bias_ready, 1)
            pool.tensor_scalar(code_bias[:, :], iota_f[:, 0:1], 0.5, 0.5, ALU.mult, ALU.add).then_inc(bias_ready, 1)

            def nonedges(nb, ks):
                for k in ks:
                    hold(pool, "pool", adj_loaded[k], 16 * (nb + 1))
                    if not (isinstance(nb, int) and nb == 0):
                        hold(pool, "pool", ordinal_ready, PREP * (nb - 1) + min(PREP, (H - 1) * K + k + 2))
                    pool.tensor_scalar(nonedge[:, k, :], adj_in[:, k, :], 0.0, None, ALU.is_equal).then_inc(nonedge_ready, 1)

            def norm(nb):
                hold(pool, "pool", stats_ready, nb + 1)
                if not (isinstance(nb, int) and nb == 0):
                    hold(pool, "pool", h32_ready, nb)
                pool.tensor_scalar(var_eps[:, :], mv[:, :, 1], EPS, None, ALU.add).then_inc(pool_step, 1)
                pool.tensor_scalar(mean_neg[:, :], mv[:, :, 0], -1.0, None, ALU.mult).then_inc(pool_step, 1)
                hold(pool, "pool", pool_step, 4 * nb + 2)
                pool.tensor_tensor(rstd[:, :], var_eps[:, :], minus_half[:, :], ALU.pow).then_inc(pool_step, 1)
                hold(pool, "pool", pool_step, 4 * nb + 3)
                pool.tensor_scalar(rstd_s[:, :], rstd[:, :], SCALE, None, ALU.mult).then_inc(pool_step, 1)
                hold(pool, "pool", pool_step, 4 * nb + 4)
                pool.tensor_tensor(shift[:, :], mean_neg[:, :], rstd_s[:, :], ALU.mult).then_inc(norm_ready, 1)

            def low_part(nb, par):
                pool.wait_ge(hi_ready, nb + 1)
                pool.tensor_tensor(h16[:, par, 1, :, :], h32[:, :, :], h16[:, par, 0, :, :], ALU.subtract).then_inc(lo_ready, 1)

            def tail_counts(nb, par):
                ROWS = K + PAIRS
                pool.wait_ge(over_ready, H * (nb + 1))
                pool.tensor_tensor(over_sum[0:ROWS, :], over[0:ROWS, 0:1], over[0:ROWS, 1:2], ALU.add).then_inc(over_summed, 1)
                hold(pool, "pool", over_summed, nb + 1)
                pool.dma_start(tail_f[0:1, 0:ROWS], over_sum[0:ROWS, :]).then_inc(tail_row, 16)
                pool.wait_ge(tail_row, 16 * (nb + 1))
                both = tail_f[0:1, 0:K].rearrange("u (p c) -> u p c", c=2)
                pool.tensor_tensor(tail_f[0:1, ROWS:], both[:, :, 0], both[:, :, 1], ALU.add).then_inc(tail_any, 1)
                pool.wait_ge(tail_any, 3 * nb + 1)
                pool.tensor_tensor(tail_f[0:1, ROWS:], tail_f[0:1, ROWS:], tail_f[0:1, K:ROWS], ALU.add).then_inc(tail_any, 1)
                hold(pool, "pool", tail_any, 3 * nb + 2)
                pool.tensor_scalar(tail_clip[0:1, :], tail_f[0:1, :], float(LIMIT - STATIC), None, ALU.min).then_inc(tail_any, 1)
                hold(pool, "pool", tail_any, 3 * nb + 3)
                pool.tensor_copy(tail_word[0:1, par, :], tail_clip[0:1, :]).then_inc(tail_loaded, 1)

            def finish(b):
                pool.wait_ge(dense_read, 4 * b + 5)
                pool.wait_ge(xT_loaded, 16 * (b + 1))
                if not (isinstance(b, int) and b == 0):
                    pool.wait_ge(stored, 16 * b)
                pool.tensor_tensor(out_sb[:, :], act_out[:, :], xT_in[:, :], ALU.add).then_inc(added, 1)
                pool.wait_ge(added, b + 2)
                pool.dma_start(outT[b], out_sb[:, :]).then_inc(stored, 16)

            norm(0)
            low_part(0, 0)
            tail_counts(0, 0)
            nonedges(1, range(K // 2))
            with pool.Fori(1, B - 1) as nb:
                par = nb & 1
                nonedges(nb, range(K // 2, K))
                norm(nb)
                low_part(nb, par)
                nonedges(nb + 1, range(K // 2))
                tail_counts(nb, par)
                finish(nb - 1)
            nonedges(B - 1, range(K // 2, K))
            norm(B - 1)
            low_part(B - 1, (B - 1) & 1)
            tail_counts(B - 1, (B - 1) & 1)
            finish(B - 2)

        @block.scalar
        def _(act):
            act.sem_inc(dense_read, 1)
            act.wait_ge(bias_ready, 3)
            act.wait_ge(const_ready, 4 + 2 * K + 1)

            def edges(nb, p):
                half, k = divmod(p, K)
                act.wait_ge(ordinal_ready, PREP * nb + p + 1)
                if not (isinstance(nb, int) and nb == 0 and p < 2):
                    act.wait_ge(number_ready, PREP * nb + p - 1)
                act.activation(valid[:, p % 2, :], ordinal_ps[:, :], ACT.Sign,
                               bias=valid_bias[:, k:k + 1]).then_inc(valid_ready, 1)

            def codes(nb, par, p):
                half, k = divmod(p, K)
                act.wait_ge(number_ready, PREP * nb + p + 1)
                if p == 0 and not (isinstance(nb, int) and nb < 2):
                    act.wait_ge(agg_done, nb - 1)
                act.activation(code[:, par, k, half * WIDTH:(half + 1) * WIDTH], number_ps[:, :], ACT.Identity,
                               bias=code_bias[:, :], scale=0.5).then_inc(code_ready, 1)
                if k == K - 1:
                    if not (isinstance(nb, int) and nb == 0):
                        act.wait_ge(over_summed, nb)
                    if half:
                        act.wait_ge(over_ready, H * nb + half)
                    act.activation(over_junk[0:K + PAIRS, :], degree_ps[0:K + PAIRS, :], ACT.Relu,
                                   bias=over_bias[0:K + PAIRS, :], scale=0.5,
                                   accum_out=over[0:K + PAIRS, half:half + 1]).then_inc(over_ready, 1)

            def make_h(nb, par):
                act.wait_ge(x_loaded, 16 * (nb + 1))
                act.wait_ge(norm_ready, nb + 1)
                if not (isinstance(nb, int) and nb == 0):
                    act.wait_ge(lo_ready, nb)
                for k in range(K):
                    last = act.activation(h32[:, k, :], x_in[:, k, :], ACT.Relu, bias=shift[:, k:k + 1],
                                          scale=rstd_s[:, k:k + 1])
                last.then_inc(h32_ready, 1)
                act.wait_ge(h32_ready, nb + 1)
                act.activation(h16[:, par, 0, :, :], h32[:, :, :], ACT.Copy).then_inc(hi_ready, 1)

            def copy_hT(b, half):
                act.wait_ge(dense_ready, 4 * b + half + 1)
                act.activation(hT[:, half * WIDTH:(half + 1) * WIDTH], dense_ps[:, :], ACT.Copy).then_inc(dense_read, 1)

            def relu_out(b, half):
                act.wait_ge(dense_ready, 4 * b + 3 + half)
                if half == 0:
                    act.wait_ge(added, b + 1)
                act.activation(act_out[:, half * WIDTH:(half + 1) * WIDTH], dense_ps[:, :], ACT.Relu,
                               bias=b_sb[:, :]).then_inc(dense_read, 1)

            def make_onehot(b, par, j):
                pair, t = j // STEPS, FROM_ACT[j % STEPS]
                (c, ordinal), = parts(t)
                k = 2 * pair + c
                if not (isinstance(b, int) and b == 0 and pair == 0):
                    act.wait_ge(gather_ready, SLOTS * b + PAIR * (pair - 1) + t)
                hold(act, "act", act_onehot_ready, PREP * b + j + 1)
                act.activation(distance[:, :], code[:, par, k, :], ACT.Abs,
                               bias=act_target[:, ordinal:ordinal + 1]).then_inc(distance_ready, 1)
                act.wait_ge(distance_ready, PREP * b + j + 1)
                act.activation(act_onehot[:, j % STEPS, :], distance[:, :], ACT.Relu, bias=1.0,
                               scale=-1.0).then_inc(act_onehot_ready, 1)

            def body(b, par, par_next, first, last):
                for p in range(PREP):
                    if not last:
                        edges(b + 1, p)
                        codes(b + 1, par_next, p)
                    if p + AHEAD_ACT < PREP:
                        make_onehot(b, par, p + AHEAD_ACT)
                    elif not last:
                        make_onehot(b + 1, par_next, p + AHEAD_ACT - PREP)
                    if not first and p < H:
                        relu_out(b - 1, p)
                    if p == STEPS or p == 2 * STEPS:
                        copy_hT(b, p // STEPS - 1)
                    if p == 11 and not last:
                        make_h(b + 1, par_next)

            make_h(0, 0)
            edges(0, 0)
            for p in range(PREP):
                if p + 1 < PREP:
                    edges(0, p + 1)
                codes(0, 0, p)
            act.sem_inc(act_onehot_ready, 1)
            for j in range(AHEAD_ACT):
                make_onehot(0, 0, j)
            act.wait_ge(w_loaded, 48)
            body(0, 0, 1, True, False)
            with act.Fori(1, B - 1) as b:
                body(b, b & 1, (b + 1) & 1, False, False)
            body(B - 1, (B - 1) & 1, 0, False, True)
            for half in range(H):
                relu_out(B - 1, half)

        @block.vector
        def _(dve):
            def stats_of(nb, k):
                if k == 0:
                    dve.wait_ge(x_loaded, 16 * (nb + 1))
                dve.bn_stats(stats[:, k, :], x_in[:, k, :]).then_inc(stats_part, 1)

            def means_of(nb, k):
                if k == 0:
                    hold(dve, "dve", stats_part, K * (nb + 1))
                    if not (isinstance(nb, int) and nb == 0):
                        hold(dve, "dve", norm_ready, nb)
                last = dve.bn_aggr(mv[:, k, :], stats[:, k, :])
                if k == K - 1:
                    last.then_inc(stats_ready, 1)

            def make_onehots(b, par, n):
                pair, t = n // PAIR, n % PAIR + 1
                if t in FROM_ACT:
                    return
                for q, (c, s) in enumerate(parts(t)):
                    k = 2 * pair + c
                    if s == (1 if c == 0 else STATIC):
                        dve.wait_ge(code_ready, PREP * b + (H - 1) * K + k + 1)
                    dve.tensor_scalar(onehot[:, onehot_index(pair, t, q) % ONEHOTS, :], code[:, par, k, :],
                                      float(CODE_AT + s), None, ALU.is_equal).then_inc(onehot_ready, 1)

            def take_max(b, par, n):
                dve.wait_ge(gather_ready, SLOTS * b + n + 1)
                if n == 0:
                    dve.tensor_scalar(agg[:, par, :], gathered[0][:, :], 0.0, None, ALU.max).then_inc(max_done, 1)
                else:
                    dve.wait_ge(max_done, SLOTS * b + n)
                    dve.tensor_tensor(agg[:, par, :], gathered[n % 2][:, :], agg[:, par, :], ALU.max).then_inc(max_done, 1)

            def tail_slot(b, par, k, n_next, s, done):
                dve.reg_add(done, done, 1)
                d = dve.snap(done)
                dve.tensor_scalar(tail_onehot[:, :], code[:, par, k, :], float(CODE_AT), slot_code[:, bass.ds(s, 1)],
                                  ALU.subtract, ALU.is_equal).then_inc(tail_onehot_ready, 1)
                dve.wait_ge(tail_gather_ready, d)
                dve.wait_ge(max_done, SLOTS * b + n_next)
                dve.tensor_tensor(agg[:, par, :], gathered[n_next % 2][:, :], agg[:, par, :], ALU.max).then_inc(tail_max_done, 1)
                hold(dve, "dve", tail_max_done, d)

            def body(b, par, par_next, last, done):
                for n in range(SLOTS):
                    pair, m = divmod(n, PAIR)
                    ahead = n + LOOKAHEAD
                    if ahead < SLOTS:
                        make_onehots(b, par, ahead)
                    elif not last:
                        make_onehots(b + 1, par_next, ahead - SLOTS)
                    take_max(b, par, n)
                    if not last and 2 * K <= n < 3 * K:
                        stats_of(b + 1, n - 2 * K)
                    if not last and 3 * K <= n < 4 * K:
                        means_of(b + 1, n - 3 * K)
                    if m == PAIR - 1:
                        tail(dve, "dve", b, par, pair, done, tail_slot)
                dve.wait_ge(max_done, SLOTS * (b + 1))
                dve.sem_inc(agg_done, 1)

            for k in range(K):
                stats_of(0, k)
            for k in range(K):
                means_of(0, k)
            for k in range(K):
                dve.wait_ge(adj_loaded[k], 16)
                dve.tensor_scalar(nonedge[:, k, :], adj_in[:, k, :], 0.0, None, ALU.is_equal).then_inc(nonedge_ready, 1)
            dve.wait_ge(w_loaded, 48)
            dve.tensor_scalar(w_sb[:, :, :], w_in[:, :, :], 1.0 / SCALE, None, ALU.mult).then_inc(w_ready, 1)
            dve.wait_ge(bias_ready, 3)
            for n in range(LOOKAHEAD):
                make_onehots(0, 0, n)
            done = dve.alloc_register("tail_slots_done")
            dve.reg_mov(done, 0)
            body(0, 0, 1, False, done)
            with dve.Fori(1, B - 1) as b:
                body(b, b & 1, (b + 1) & 1, False, done)
            body(B - 1, (B - 1) & 1, 0, True, done)
            dve.wait_ge(xT_loaded, 16 * B)
            dve.wait_ge(stored, 16 * (B - 1))
            for half in range(H):
                cols = slice(half * WIDTH, (half + 1) * WIDTH)
                dve.wait_ge(dense_read, 4 * B + half)
                dve.tensor_tensor(out_sb[:, cols], act_out[:, cols], xT_in[:, cols], ALU.add).then_inc(last_added, 1)

        @block.tensor
        def _(pe):
            pe.wait_ge(const_ready, 4 + 2 * K)

            def order(nb, p):
                half, k = divmod(p, K)
                cols = slice(half * WIDTH, (half + 1) * WIDTH)
                pe.wait_ge(nonedge_ready, K * nb + k + 1)
                if not (isinstance(nb, int) and nb == 0 and p == 0):
                    pe.wait_ge(valid_ready, PREP * nb + p)
                if k:
                    pe.matmul(ordinal_ps[:, :], count_rest[:, :], nonedge[:, k - 1, cols], start=False, stop=False,
                              skip_group_check=True)
                pe.matmul(ordinal_ps[:, :], count_here[:, :], nonedge[:, k, cols], start=(k == 0), stop=True,
                          skip_group_check=True).then_inc(ordinal_ready, 1)

            def renumber(nb, p):
                half, k = divmod(p, K)
                pe.wait_ge(valid_ready, PREP * nb + p + 1)
                if not (isinstance(nb, int) and nb == 0 and p == 0):
                    pe.wait_ge(code_ready, PREP * nb + p)
                if k == 0 and not (isinstance(nb, int) and nb == 0 and half == 0):
                    pe.wait_ge(over_ready, H * nb + half)
                pe.matmul(degree_ps[:, :], pick_row[:, k, :], valid[:, p % 2, :], start=(k == 0), stop=(k == K - 1),
                          skip_group_check=True)
                pe.matmul(number_ps[:, :], number[:, :], valid[:, p % 2, :], start=True,
                          stop=True).then_inc(number_ready, 1)

            def products(buf, par, k, hot, start, stop):
                for part in range(2):
                    for half in range(H):
                        cols = slice(half * WIDTH, (half + 1) * WIDTH)
                        last = pe.matmul(buf[:, cols], h16[:, par, part, k, :], hot[:, cols],
                                         start=(start and part == 0), stop=(stop and part == 1))
                return last

            def hot_of(b, pair, t, q):
                if t in FROM_ACT:
                    j = pair * STEPS + FROM_ACT.index(t)
                    pe.wait_ge(act_onehot_ready, PREP * b + j + 2)
                    return act_onehot[:, j % STEPS, :]
                i = onehot_index(pair, t, q)
                pe.wait_ge(onehot_ready, PAIRS * len(BY_DVE) * b + i + 1)
                return onehot[:, i % ONEHOTS, :]

            def gather(b, par, n, clash=False):
                pair, t = n // PAIR, n % PAIR + 1
                if n > 1 or not (isinstance(b, int) and b == 0):
                    pe.wait_ge(max_done, SLOTS * b + n - 1)
                taken = parts(t)[:1] if clash else parts(t)
                for q, (c, s) in enumerate(taken):
                    last = products(gathered[n % 2], par, 2 * pair + c, hot_of(b, pair, t, q), q == 0,
                                    q == len(taken) - 1)
                last.then_inc(gather_ready, 1)

            def tail_slot(b, par, k, n_next, s, done):
                pe.reg_add(done, done, 1)
                d = pe.snap(done)
                pe.wait_ge(max_done, SLOTS * b + n_next - 1)
                pe.wait_ge(tail_onehot_ready, d)
                products(gathered[n_next % 2], par, k, tail_onehot, True, True).then_inc(tail_gather_ready, 1)
                hold(pe, "pe", tail_max_done, d)

            def transpose_h(b, par, half):
                pe.wait_ge(dense_read, 4 * b + half + 1)
                chunks = WIDTH // P
                for q in range(chunks):
                    for part in range(2):
                        last = pe.matmul(dense_ps[:, q * P:(q + 1) * P], h16[:, par, part, half * chunks + q, :],
                                         ident[:, :], start=(part == 0), stop=(part == 1))
                last.then_inc(dense_ready, 1)

            def dense(b, par, half):
                cols = slice(half * WIDTH, (half + 1) * WIDTH)
                if half == 0:
                    pe.wait_ge(agg_done, b + 1)
                pe.wait_ge(dense_read, 4 * b + 3 + half)
                pe.matmul(dense_ps[:, :], w_sb[:, 0, :], hT[:, cols], start=True, stop=False)
                pe.matmul(dense_ps[:, :], w_sb[:, 1, :], agg[:, par, cols], start=False, stop=True).then_inc(dense_ready, 1)

            def body(b, par, par_next, first, last, done):
                pe.wait_ge(lo_ready, b + 1)
                for n in range(SLOTS):
                    pair, t = n // PAIR, n % PAIR + 1
                    if len(parts(t)) == 1:
                        gather(b, par, n)
                    elif len(parts(t - 1)) == 1:
                        if pair == 0:
                            hold(pe, "pe", tail_loaded, b + 1)
                        clashes = pe.value_load(tail_word[0:1, par, K + pair:K + pair + 1], min_val=0,
                                                max_val=LIMIT - STATIC)
                        with pe.If(clashes > 0):
                            for i in range(SHARED):
                                gather(b, par, n + i, clash=True)
                        with pe.Else():
                            for i in range(SHARED):
                                gather(b, par, n + i)
                    if not last:
                        if t in ORDER_AT:
                            order(b + 1, pair * STEPS + ORDER_AT.index(t))
                        if t in RENUMBER_AT:
                            renumber(b + 1, pair * STEPS + RENUMBER_AT.index(t))
                    if not first and pair == 0 and t in ORDER_AT[:H]:
                        dense(b - 1, 1 - par, ORDER_AT.index(t))
                    if t == 3 and 1 <= pair <= H:
                        transpose_h(b, par, pair - 1)
                    if t == PAIR:
                        tail(pe, "pe", b, par, pair, done, tail_slot)

            order(0, 0)
            for p in range(PREP):
                if p + 1 < PREP:
                    order(0, p + 1)
                renumber(0, p)
            pe.wait_ge(w_ready, 1)
            done = pe.alloc_register("tail_slots_done")
            pe.reg_mov(done, 0)
            body(0, 0, 1, True, False, done)
            with pe.Fori(1, B - 1) as b:
                body(b, b & 1, (b + 1) & 1, False, False, done)
            body(B - 1, (B - 1) & 1, 0, False, True, done)
            for half in range(H):
                dense(B - 1, (B - 1) & 1, half)


def kernel(x, adj, L0_gnn_W, L0_gnn_b):
    import numpy as np
    import concourse.bacc as bacc
    from concourse.bass_utils import run_bass_kernel_spmd

    x = np.asarray(x)
    arrays = {
        "x": np.ascontiguousarray(x),
        "x_by_channel": np.ascontiguousarray(x.transpose(0, 2, 1)),
        "adj_by_source": np.ascontiguousarray(np.asarray(adj).transpose(0, 2, 1)),
        "W": np.ascontiguousarray(L0_gnn_W),
        "b": np.ascontiguousarray(L0_gnn_b),
    }
    nc = bacc.Bacc("TRN2", target_bir_lowering=False, num_devices=1)
    args = [nc.dram_tensor(name, a.shape, mybir.dt.from_np(a.dtype), kind="ExternalInput").ap()
            for name, a in arrays.items()]
    B, N, C = x.shape
    out = nc.dram_tensor("out_by_channel", (B, C, N), F32, kind="ExternalOutput").ap()
    adj_preln_kernel(nc, *args, out)
    r = run_bass_kernel_spmd(nc, [arrays], core_ids=[0])
    return np.ascontiguousarray(r.results[0]["out_by_channel"].transpose(0, 2, 1))
```

```python
from contextlib import ExitStack

import concourse.bass as bass
from concourse import mybir

F32 = mybir.dt.float32
F16 = mybir.dt.float16
I32 = mybir.dt.int32
ALU = mybir.AluOpType
ACT = mybir.ActivationFunctionType

P = 128
LIMIT = 25
EPS = 1e-5
SCALE = 4096.0
STATIC = 8
EDGE = 1050
MARK = 512
CODE_AT = MARK // 2
PAIR = 13
SHARED = 2 * STATIC - PAIR
FROM_ACT = (4, 5, 10, 12)
AHEAD_ACT = 5
ORDINALS = STATIC + 32
EXTRA = PAIR - STATIC
LOOKAHEAD = 2
ONEHOTS = 8
VALIDS = 4
WIDTH = 512


def adj_preln_kernel(nc, x, xT, adjT, W, b, outT):
    B, N, C = x.shape
    K = N // P
    H = N // WIDTH
    PREP = H * K
    PAIRS = K // 2
    SLOTS = PAIRS * PAIR
    BY_ACT = len(FROM_ACT)
    ORDER_AT = {2 + p * (SLOTS - 10) // PREP: p for p in range(PREP)}
    RENUMBER_AT = {n + 1: p for n, p in ORDER_AT.items()}
    DENSE_AT = {1: 0, 4: 1}
    TRANSPOSE_AT = {PAIR * (1 + half) + 2: half for half in range(H)}
    STATS_AT = {K + k: k for k in range(K)}
    MEANS_AT = {2 * K + k: k for k in range(K)}
    MAKE_H_AT = {3 * K + 2 + k: k for k in range(K)}
    AHEAD_NONEDGES = K // 4
    assert len(ORDER_AT) == PREP and H == 2

    WORD_STEPS = 16
    WORD_MAX = 5 + 8 * 5 + 64 + (LIMIT - STATIC) * (128 + 4096)

    def parts(t):
        return [(c, s) for c, s in ((0, t), (1, PAIR + 1 - t)) if s <= STATIC]

    BY_DVE = [(t, q) for t in range(1, PAIR + 1) if t not in FROM_ACT for q in range(len(parts(t)))]
    assert PAIRS * len(BY_DVE) % ONEHOTS == 0

    def onehot_index(pair, t, q):
        return pair * len(BY_DVE) + BY_DVE.index((t, q))

    ctx = ExitStack()
    with ctx:
        def sb(name, shape, dt):
            return ctx.enter_context(nc.sbuf_tensor(name, shape, dt))

        def sem(name):
            return ctx.enter_context(nc.semaphore(name))

        adj_in = sb("adj_in", [P, K, N], I32)
        nonedge = sb("nonedge", [P, K, N], F16)
        valid = sb("valid", [P, VALIDS, WIDTH], F16)
        code = sb("code", [P, 2, K, N], F16)
        onehot = sb("onehot", [P, ONEHOTS, N], F16)
        tail_onehot = sb("tail_onehot", [P, N], F16)
        extra_onehot = sb("extra_onehot", [P, 2, N], F16)
        x_in = sb("x_in", [P, K, C], F32)
        stats = sb("stats", [P, K, 6], F32)
        mv = sb("mv", [P, K, 2], F32)
        var_eps = sb("var_eps", [P, K], F32)
        rstd = sb("rstd", [P, K], F32)
        rstd_s = sb("rstd_s", [P, K], F32)
        mean_neg = sb("mean_neg", [P, K], F32)
        shift = sb("shift", [P, K], F32)
        h32 = sb("h32", [P, K, C], F32)
        h16 = sb("h16", [P, 2, 2, K, C], F16)
        hT = sb("hT", [P, N], F32)
        agg = sb("agg", [P, 2, N], F32)
        act_onehot = sb("act_onehot", [P, BY_ACT, N], F16)
        distance = sb("distance", [P, N], F16)
        xT_in = sb("xT_in", [P, N], F32)
        act_out = sb("act_out", [P, N], F32)
        out_sb = sb("out_sb", [P, N], F32)
        over = sb("over", [P, 2], F32)
        over_sum = sb("over_sum", [P, 1], F32)
        tail_f = sb("tail_f", [1, K + PAIRS], F32)
        over_a, over_b, fits_a, fits_b, clash, clash_bit, flag, flag_bit = (
            sb(name, [1, PAIRS], F32)
            for name in ("over_a", "over_b", "fits_a", "fits_b", "clash", "clash_bit", "flag", "flag_bit"))
        pair_word = sb("pair_word", [1, PAIRS + 1], F32)
        over_junk = sb("over_junk", [P, WIDTH], F16)
        tail_word = sb("tail_word", [1, 2, PAIRS + 1], I32)
        w_in = sb("w_in", [P, 2, C], F32)
        w_sb = sb("w_sb", [P, 2, C], F32)
        b_sb = sb("b_sb", [P, 1], F32)
        count_here = sb("count_here", [P, P], F16)
        count_rest = sb("count_rest", [P, P], F16)
        number = sb("number", [P, P], F16)
        ident = sb("ident", [P, P], F16)
        pick_row = sb("pick_row", [P, K, P], F16)
        iota_i = sb("iota_i", [P, K], I32)
        iota_s = sb("iota_s", [P, ORDINALS], I32)
        iota_f = sb("iota_f", [P, K], F32)
        valid_bias = sb("valid_bias", [P, K], F32)
        code_bias = sb("code_bias", [P, 1], F32)
        over_bias = sb("over_bias", [P, 1], F32)
        slot_code = sb("slot_code", [P, ORDINALS], F32)
        act_target = sb("act_target", [P, ORDINALS], F32)
        minus_half = sb("minus_half", [P, K], F32)

        gathered = [ctx.enter_context(nc.psum_tensor(f"gathered{i}", [P, N], F32)) for i in range(2)]
        ordinal_ps = ctx.enter_context(nc.psum_tensor("ordinal_ps", [P, WIDTH], F32))
        number_ps = ctx.enter_context(nc.psum_tensor("number_ps", [P, WIDTH], F32))
        degree_ps = ctx.enter_context(nc.psum_tensor("degree_ps", [P, WIDTH], F32))
        dense_ps = ctx.enter_context(nc.psum_tensor("dense_ps", [P, WIDTH], F32))

        adj_loaded = [sem(f"adj_loaded{k}") for k in range(K)]
        x_loaded = sem("x_loaded")
        xT_loaded = sem("xT_loaded")
        w_loaded = sem("w_loaded")
        const_set = sem("const_set")
        const_ready = sem("const_ready")
        flag_bit_set = sem("flag_bit_set")
        bias_ready = sem("bias_ready")
        w_ready = sem("w_ready")
        nonedge_ready = sem("nonedge_ready")
        ordinal_ready = sem("ordinal_ready")
        valid_ready = sem("valid_ready")
        number_ready = sem("number_ready")
        code_ready = sem("code_ready")
        over_ready = sem("over_ready")
        over_summed = sem("over_summed")
        tail_row = sem("tail_row")
        tail_step = sem("tail_step")
        distance_ready = sem("distance_ready")
        act_onehot_ready = sem("act_onehot_ready")
        last_added = sem("last_added")
        last_stored = sem("last_stored")
        tail_loaded = sem("tail_loaded")
        onehot_ready = sem("onehot_ready")
        gather_ready = sem("gather_ready")
        max_done = sem("max_done")
        extra_ready = sem("extra_ready")
        tail_onehot_ready = sem("tail_onehot_ready")
        tail_gather_ready = sem("tail_gather_ready")
        tail_max_done = sem("tail_max_done")
        agg_done = sem("agg_done")
        stats_part = sem("stats_part")
        stats_ready = sem("stats_ready")
        pool_step = sem("pool_step")
        norm_ready = sem("norm_ready")
        h32_ready = sem("h32_ready")
        hi_ready = sem("hi_ready")
        lo_ready = sem("lo_ready")
        dense_ready = sem("dense_ready")
        dense_read = sem("dense_read")
        added = sem("added")
        stored = sem("stored")

        passed = {name: sem(f"{name}_passed") for name in ("pool", "dve", "pe", "act")}

        def hold(eng, name, semaphore, value):
            eng.wait_ge(semaphore, value)
            eng.sem_inc(passed[name], 1)

        class Word:

            def __init__(self, eng, par, pair):
                word = eng.value_load(tail_word[0:1, par, pair:pair + 1], min_val=0, max_val=WORD_MAX)
                self.extra = (word & 7, (word >> 3) & 7)
                self.clash = (word >> 6) & 1
                self.over = ((word >> 7) & 31, (word >> 12) & 31)

        def flags_of(eng, name, b, par):
            hold(eng, name, tail_loaded, b + 1)
            return eng.value_load(tail_word[0:1, par, PAIRS:PAIRS + 1], min_val=0, max_val=2 ** PAIRS - 1)

        def tail(eng, name, b, par, pair, word, done, tail_slot):
            n_next = PAIR * (pair + 1)
            (extra_a, extra_b), (over_a, over_b), c = word.extra, word.over, word.clash
            with eng.If(over_a + over_b + c - extra_a - extra_b > 0):
                with eng.If(over_a - extra_a > 0):
                    with eng.Fori(STATIC + 1 + extra_a, STATIC + 1 + over_a) as s:
                        tail_slot(b, par, 2 * pair, n_next, s, done)
                with eng.If(over_b + c - extra_b > 0):
                    with eng.Fori(STATIC + 1 + extra_b - c * SHARED, STATIC + 1 + over_b) as s:
                        tail_slot(b, par, 2 * pair + 1, n_next, s, done)
                eng.sem_inc(passed[name], 1)

        def ordinal_first(half):
            return (ordinal_ps, dense_ps)[half][:, :]

        def degree_first(half):
            return (degree_ps[0:K + PAIRS, :], gathered[0][0:K + PAIRS, 0:WIDTH])[half]

        def number_first(half):
            return (number_ps[:, :], gathered[0][:, WIDTH:])[half]

        block = ctx.enter_context(nc.Block())

        @block.sync
        def _(sp):
            def load(nb, first):
                if not first:
                    sp.wait_ge(hi_ready, nb)
                    sp.wait_ge(stats_ready, nb)
                sp.dma_start(x_in[:, :, :], x[nb].rearrange("(k p) c -> p k c", p=P)).then_inc(x_loaded, 16)
                for k in range(K):
                    if not first:
                        sp.wait_ge(nonedge_ready, K * (nb - 1) + k + 1)
                    sp.dma_start(adj_in[:, k, :], adjT[nb, k * P:(k + 1) * P, :]).then_inc(adj_loaded[k], 16)

            def load_xT(nb, first):
                if not first:
                    sp.wait_ge(added, nb + 1)
                sp.dma_start(xT_in[:, :], xT[nb]).then_inc(xT_loaded, 16)

            load(0, True)
            for part in range(2):
                sp.dma_start(w_in[:, part, :], W[part * C:(part + 1) * C, :]).then_inc(w_loaded, 16)
            sp.dma_start(b_sb[:, :], b.rearrange("(o u) -> o u", u=1)).then_inc(w_loaded, 16)
            load_xT(0, True)
            load(1, False)
            with sp.Fori(2, B) as nb:
                load(nb, False)
                load_xT(nb - 1, False)
            load_xT(B - 1, False)
            for half in range(H):
                cols = slice(half * WIDTH, (half + 1) * WIDTH)
                sp.wait_ge(last_added, half + 1)
                sp.dma_start(outT[B - 1, :, cols], out_sb[:, cols]).then_inc(last_stored, 16)
            sp.wait_ge(stored, 16 * (B - 1))
            sp.wait_ge(last_stored, 16 * H)

        @block.gpsimd
        def _(pool):
            pool.sem_inc(added, 1)
            n_set = 0
            for t, v in ((count_here, 1.0), (count_rest, 1.0), (number, 1.0), (ident, 0.0), (pick_row, 0.0),
                         (minus_half, -0.5), (over_bias, float(P - PAIR))):
                pool.memset(t[:, :] if len(t.shape) == 2 else t[:, :, :], v).then_inc(const_set, 1)
                n_set += 1
            pool.iota(iota_i[:, :], [[P, K]], base=0, channel_multiplier=1).then_inc(const_set, 1)
            pool.iota(iota_s[:, :], [[1, ORDINALS]], base=0, channel_multiplier=0).then_inc(const_set, 1)
            n_set += 2
            pool.wait_ge(const_set, n_set)
            for t, sign, base in ((count_here, 1, 0), (number, 1, 0), (count_rest, -1, -1)):
                pool.affine_select(out=t[:, :], in_=t[:, :], compare_op=ALU.is_ge, fill=0.0, base=base,
                                   pattern=[[sign, P]], channel_multiplier=-sign).then_inc(const_set, 1)
            pool.tensor_copy(iota_f[:, :], iota_i[:, :]).then_inc(const_set, 1)
            pool.tensor_copy(slot_code[:, :], iota_s[:, :]).then_inc(const_set, 1)
            n_set += 5
            pool.wait_ge(const_set, n_set)
            for t, diagonal in ((count_here, 1.0 - EDGE), (count_rest, float(EDGE)), (number, 1.0 + MARK),
                                (ident, 1.0)):
                pool.affine_select(out=t[:, :], in_=t[:, :], compare_op=ALU.not_equal, fill=diagonal, base=0,
                                   pattern=[[-1, P]], channel_multiplier=1).then_inc(const_ready, 1)
            for k in range(K):
                pool.memset(pick_row[:, k, k:k + 1], 1.0).then_inc(const_ready, 1)
                pool.memset(pick_row[:, k, K + k // 2:K + k // 2 + 1], 1.0).then_inc(const_ready, 1)
            pool.memset(over_bias[0:K, :], P / 2 - STATIC).then_inc(const_ready, 1)
            for pair in range(PAIRS):
                pool.memset(flag_bit[0:1, pair:pair + 1], 2.0 ** pair).then_inc(flag_bit_set, 1)
            pool.wait_ge(flag_bit_set, PAIRS)
            pool.tensor_scalar(valid_bias[:, :], iota_f[:, :], -1.0, LIMIT - 0.5, ALU.mult, ALU.add).then_inc(bias_ready, 1)
            pool.tensor_scalar(act_target[:, :], slot_code[:, :], -1.0, -float(CODE_AT), ALU.mult, ALU.add).then_inc(bias_ready, 1)
            pool.tensor_scalar(code_bias[:, :], iota_f[:, 0:1], 0.5, 0.5, ALU.mult, ALU.add).then_inc(bias_ready, 1)

            def nonedges(nb, ks):
                for k in ks:
                    hold(pool, "pool", adj_loaded[k], 16 * (nb + 1))
                    if not (isinstance(nb, int) and nb == 0):
                        hold(pool, "pool", ordinal_ready, PREP * (nb - 1) + min(PREP, (H - 1) * K + k + 2))
                    pool.tensor_scalar(nonedge[:, k, :], adj_in[:, k, :], 0.0, None, ALU.is_equal).then_inc(nonedge_ready, 1)

            def norm(nb):
                hold(pool, "pool", stats_ready, nb + 1)
                if not (isinstance(nb, int) and nb == 0):
                    hold(pool, "pool", h32_ready, nb)
                pool.tensor_scalar(var_eps[:, :], mv[:, :, 1], EPS, None, ALU.add).then_inc(pool_step, 1)
                pool.tensor_scalar(mean_neg[:, :], mv[:, :, 0], -1.0, None, ALU.mult).then_inc(pool_step, 1)
                hold(pool, "pool", pool_step, 4 * nb + 2)
                pool.tensor_tensor(rstd[:, :], var_eps[:, :], minus_half[:, :], ALU.pow).then_inc(pool_step, 1)
                hold(pool, "pool", pool_step, 4 * nb + 3)
                pool.tensor_scalar(rstd_s[:, :], rstd[:, :], SCALE, None, ALU.mult).then_inc(pool_step, 1)
                hold(pool, "pool", pool_step, 4 * nb + 4)
                pool.tensor_tensor(shift[:, :], mean_neg[:, :], rstd_s[:, :], ALU.mult).then_inc(norm_ready, 1)

            def low_part(nb, par):
                pool.wait_ge(hi_ready, nb + 1)
                pool.tensor_tensor(h16[:, par, 1, :, :], h32[:, :, :], h16[:, par, 0, :, :], ALU.subtract).then_inc(lo_ready, 1)

            def tail_counts(nb, par):
                ROWS = K + PAIRS
                pool.wait_ge(over_ready, H * (nb + 1))
                pool.tensor_tensor(over_sum[0:ROWS, :], over[0:ROWS, 0:1], over[0:ROWS, 1:2], ALU.add).then_inc(over_summed, 1)
                hold(pool, "pool", over_summed, nb + 1)
                pool.dma_start(tail_f[0:1, 0:ROWS], over_sum[0:ROWS, :]).then_inc(tail_row, 16)
                hold(pool, "pool", tail_row, 16 * (nb + 1))
                first, second = (tail_f[0:1, 0:K].rearrange("u (p c) -> u p c", c=2)[:, :, c] for c in range(2))
                clashes = tail_f[0:1, K:ROWS]
                step = [0]

                def small(op, *args):
                    op(*args).then_inc(tail_step, 1)
                    step[0] += 1

                def written():
                    hold(pool, "pool", tail_step, WORD_STEPS * nb + step[0])

                most = float(LIMIT - STATIC)
                small(pool.tensor_scalar, clash[:, :], clashes, 1.0, None, ALU.min)
                small(pool.tensor_scalar, over_a[:, :], first, most, 128.0, ALU.min, ALU.mult)
                small(pool.tensor_scalar, over_b[:, :], second, most, 4096.0, ALU.min, ALU.mult)
                small(pool.tensor_scalar, clash_bit[:, :], clashes, 1.0, 64.0, ALU.min, ALU.mult)
                small(pool.tensor_scalar, fits_a[:, :], first, float(EXTRA), None, ALU.min)
                small(pool.tensor_scalar, fits_b[:, :], second, float(EXTRA), 8.0, ALU.min, ALU.mult)
                written()
                small(pool.tensor_tensor, over_a[:, :], over_a[:, :], over_b[:, :], ALU.add)
                small(pool.tensor_scalar, clash[:, :], clash[:, :], -1.0, 1.0, ALU.mult, ALU.add)
                small(pool.tensor_tensor, fits_a[:, :], fits_a[:, :], fits_b[:, :], ALU.add)
                written()
                small(pool.tensor_tensor, over_a[:, :], over_a[:, :], clash_bit[:, :], ALU.add)
                small(pool.tensor_tensor, fits_a[:, :], fits_a[:, :], clash[:, :], ALU.mult)
                written()
                small(pool.tensor_scalar, flag[:, :], over_a[:, :], 1.0, None, ALU.min)
                small(pool.tensor_tensor, pair_word[0:1, 0:PAIRS], over_a[:, :], fits_a[:, :], ALU.add)
                written()
                small(pool.tensor_tensor, flag[:, :], flag[:, :], flag_bit[:, :], ALU.mult)
                written()
                small(pool.tensor_tensor, flag[:, 0:2], flag[:, 0:2], flag[:, 2:4], ALU.add)
                written()
                small(pool.tensor_tensor, pair_word[0:1, PAIRS:], flag[:, 0:1], flag[:, 1:2], ALU.add)
                written()
                assert step[0] == WORD_STEPS and PAIRS == 4
                pool.tensor_copy(tail_word[0:1, par, :], pair_word[0:1, :]).then_inc(tail_loaded, 1)

            def finish(b):
                pool.wait_ge(dense_read, 4 * b + 5)
                pool.wait_ge(xT_loaded, 16 * (b + 1))
                if not (isinstance(b, int) and b == 0):
                    pool.wait_ge(stored, 16 * b)
                pool.tensor_tensor(out_sb[:, :], act_out[:, :], xT_in[:, :], ALU.add).then_inc(added, 1)
                pool.wait_ge(added, b + 2)
                pool.dma_start(outT[b], out_sb[:, :]).then_inc(stored, 16)

            norm(0)
            low_part(0, 0)
            tail_counts(0, 0)
            nonedges(1, range(K))
            with pool.Fori(1, B - 1) as nb:
                par = nb & 1
                norm(nb)
                low_part(nb, par)
                nonedges(nb + 1, range(AHEAD_NONEDGES))
                tail_counts(nb, par)
                nonedges(nb + 1, range(AHEAD_NONEDGES, K))
                finish(nb - 1)
            norm(B - 1)
            low_part(B - 1, (B - 1) & 1)
            tail_counts(B - 1, (B - 1) & 1)
            finish(B - 2)

        @block.scalar
        def _(act):
            act.sem_inc(dense_read, 1)
            act.wait_ge(bias_ready, 3)
            act.wait_ge(const_ready, 4 + 2 * K + 1)

            def edges(nb, p):
                half, k = divmod(p, K)
                act.wait_ge(ordinal_ready, PREP * nb + p + 1)
                if not (isinstance(nb, int) and nb == 0 and p < VALIDS):
                    act.wait_ge(number_ready, PREP * nb + p - VALIDS + 1)
                act.activation(valid[:, p % VALIDS, :], ordinal_ps[:, :], ACT.Sign,
                               bias=valid_bias[:, k:k + 1]).then_inc(valid_ready, 1)

            def codes(nb, par, p):
                half, k = divmod(p, K)
                act.wait_ge(number_ready, PREP * nb + p + 1)
                if p == 0 and not (isinstance(nb, int) and nb < 2):
                    act.wait_ge(agg_done, nb - 1)
                act.activation(code[:, par, k, half * WIDTH:(half + 1) * WIDTH], number_ps[:, :], ACT.Identity,
                               bias=code_bias[:, :], scale=0.5).then_inc(code_ready, 1)
                if k == K - 1:
                    count_over(nb, half, degree_ps[0:K + PAIRS, :])

            def count_over(nb, half, degrees):
                if not (isinstance(nb, int) and nb == 0):
                    act.wait_ge(over_summed, nb)
                if half:
                    act.wait_ge(over_ready, H * nb + half)
                act.activation(over_junk[0:K + PAIRS, :], degrees, ACT.Relu,
                               bias=over_bias[0:K + PAIRS, :], scale=0.5,
                               accum_out=over[0:K + PAIRS, half:half + 1]).then_inc(over_ready, 1)

            def edges_first(p):
                k, half = divmod(p, H)
                act.wait_ge(ordinal_ready, p + 1)
                if p >= VALIDS:
                    act.wait_ge(number_ready, p - VALIDS + 1)
                act.activation(valid[:, p % VALIDS, :], ordinal_first(half), ACT.Sign,
                               bias=valid_bias[:, k:k + 1]).then_inc(valid_ready, 1)

            def make_h(nb, par, k):
                if k == 0:
                    act.wait_ge(x_loaded, 16 * (nb + 1))
                    act.wait_ge(norm_ready, nb + 1)
                    if not (isinstance(nb, int) and nb == 0):
                        act.wait_ge(lo_ready, nb)
                last = act.activation(h32[:, k, :], x_in[:, k, :], ACT.Relu, bias=shift[:, k:k + 1],
                                      scale=rstd_s[:, k:k + 1])
                if k < K - 1:
                    return
                last.then_inc(h32_ready, 1)
                act.wait_ge(h32_ready, nb + 1)
                act.activation(h16[:, par, 0, :, :], h32[:, :, :], ACT.Copy).then_inc(hi_ready, 1)

            def copy_hT(b, half):
                act.wait_ge(dense_ready, 4 * b + half + 1)
                act.activation(hT[:, half * WIDTH:(half + 1) * WIDTH], dense_ps[:, :], ACT.Copy).then_inc(dense_read, 1)

            def relu_out(b, half):
                act.wait_ge(dense_ready, 4 * b + 3 + half)
                if half == 0:
                    act.wait_ge(added, b + 1)
                act.activation(act_out[:, half * WIDTH:(half + 1) * WIDTH], dense_ps[:, :], ACT.Relu,
                               bias=b_sb[:, :]).then_inc(dense_read, 1)

            def make_onehot(b, par, j):
                pair, t = j // BY_ACT, FROM_ACT[j % BY_ACT]
                (c, ordinal), = parts(t)
                k = 2 * pair + c
                if not (isinstance(b, int) and b == 0 and pair == 0):
                    act.wait_ge(gather_ready, SLOTS * b + PAIR * (pair - 1) + t)
                hold(act, "act", act_onehot_ready, PAIRS * BY_ACT * b + j + 1)
                act.activation(distance[:, :], code[:, par, k, :], ACT.Abs,
                               bias=act_target[:, ordinal:ordinal + 1]).then_inc(distance_ready, 1)
                act.wait_ge(distance_ready, PAIRS * BY_ACT * b + j + 1)
                act.activation(act_onehot[:, j % BY_ACT, :], distance[:, :], ACT.Relu, bias=1.0,
                               scale=-1.0).then_inc(act_onehot_ready, 1)

            ACT_AT = {(j // BY_ACT) * PAIR + FROM_ACT[j % BY_ACT] - 1 - AHEAD_ACT: j for j in range(PAIRS * BY_ACT)}

            def body(b, par, par_next, first, last):
                for n in range(SLOTS):
                    if not last and n in ORDER_AT:
                        edges(b + 1, ORDER_AT[n])
                    if not last and n in RENUMBER_AT:
                        codes(b + 1, par_next, RENUMBER_AT[n])
                    if n in ACT_AT:
                        make_onehot(b, par, ACT_AT[n])
                    elif not last and n - SLOTS in ACT_AT:
                        make_onehot(b + 1, par_next, ACT_AT[n - SLOTS])
                    if not first and n in DENSE_AT:
                        relu_out(b - 1, DENSE_AT[n])
                    if n in TRANSPOSE_AT:
                        copy_hT(b, TRANSPOSE_AT[n])
                    if n in MAKE_H_AT and not last:
                        make_h(b + 1, par_next, MAKE_H_AT[n])

            for p in range(H):
                edges_first(p)
            for k in range(K):
                make_h(0, 0, k)
            for p in range(H, PREP):
                edges_first(p)
            act.wait_ge(number_ready, PREP)
            for half in range(H):
                count_over(0, half, degree_first(half))
            act.sem_inc(act_onehot_ready, 1)
            for n in range(-AHEAD_ACT, 0):
                if n in ACT_AT:
                    make_onehot(0, 0, ACT_AT[n])
            act.wait_ge(w_loaded, 48)
            body(0, 0, 1, True, False)
            with act.Fori(1, B - 1) as b:
                body(b, b & 1, (b + 1) & 1, False, False)
            body(B - 1, (B - 1) & 1, 0, False, True)
            for half in range(H):
                relu_out(B - 1, half)

        @block.vector
        def _(dve):
            def stats_of(nb, k):
                if k == 0:
                    dve.wait_ge(x_loaded, 16 * (nb + 1))
                dve.bn_stats(stats[:, k, :], x_in[:, k, :]).then_inc(stats_part, 1)

            def means_of(nb, k):
                if k == 0:
                    hold(dve, "dve", stats_part, K * (nb + 1))
                    if not (isinstance(nb, int) and nb == 0):
                        hold(dve, "dve", norm_ready, nb)
                last = dve.bn_aggr(mv[:, k, :], stats[:, k, :])
                if k == K - 1:
                    last.then_inc(stats_ready, 1)

            def make_onehots(b, par, n):
                pair, t = n // PAIR, n % PAIR + 1
                if t in FROM_ACT:
                    return
                for q, (c, s) in enumerate(parts(t)):
                    k = 2 * pair + c
                    if s == (1 if c == 0 else STATIC):
                        dve.wait_ge(code_ready, H * (k + 1) if isinstance(b, int) and b == 0
                                    else PREP * b + (H - 1) * K + k + 1)
                    dve.tensor_scalar(onehot[:, onehot_index(pair, t, q) % ONEHOTS, :], code[:, par, k, :],
                                      float(CODE_AT + s), None, ALU.is_equal).then_inc(onehot_ready, 1)

            def take_max(b, par, n):
                dve.wait_ge(gather_ready, SLOTS * b + n + 1)
                if n == 0:
                    dve.tensor_scalar(agg[:, par, :], gathered[0][:, :], 0.0, None, ALU.max).then_inc(max_done, 1)
                else:
                    dve.wait_ge(max_done, SLOTS * b + n)
                    dve.tensor_tensor(agg[:, par, :], gathered[n % 2][:, :], agg[:, par, :], ALU.max).then_inc(max_done, 1)

            def tail_slot(b, par, k, n_next, s, done):
                dve.reg_add(done, done, 1)
                d = dve.snap(done)
                dve.tensor_scalar(tail_onehot[:, :], code[:, par, k, :], float(CODE_AT), slot_code[:, bass.ds(s, 1)],
                                  ALU.subtract, ALU.is_equal).then_inc(tail_onehot_ready, 1)
                dve.wait_ge(tail_gather_ready, d)
                dve.wait_ge(max_done, SLOTS * b + n_next)
                dve.tensor_tensor(agg[:, par, :], gathered[n_next % 2][:, :], agg[:, par, :], ALU.max).then_inc(tail_max_done, 1)
                hold(dve, "dve", tail_max_done, d)

            def make_extra(par, pair, t, extras):
                c, s = (1, PAIR + 1 - t) if t <= EXTRA else (0, t)
                dve.reg_add(extras, extras, 1)
                dve.tensor_scalar(extra_onehot[:, t % 2, :], code[:, par, 2 * pair + c, :], float(CODE_AT + s), None,
                                  ALU.is_equal).then_inc(extra_ready, 1)

            def body(b, par, par_next, last, done, extras):
                def step(n):
                    ahead = n + LOOKAHEAD
                    if ahead < SLOTS:
                        make_onehots(b, par, ahead)
                    elif not last:
                        make_onehots(b + 1, par_next, ahead - SLOTS)
                    take_max(b, par, n)
                    if not last and n in STATS_AT:
                        stats_of(b + 1, STATS_AT[n])
                    if not last and n in MEANS_AT:
                        means_of(b + 1, MEANS_AT[n])

                flags = flags_of(dve, "dve", b, par)
                for pair in range(PAIRS):
                    def steps(first, last_t):
                        for t in range(first, last_t + 1):
                            step(PAIR * pair + t - 1)

                    def extra(t):
                        make_extra(par, pair, t, extras)

                    with dve.If((flags >> pair) & 1 > 0):
                        word = Word(dve, par, pair)
                        extra_a, extra_b = word.extra
                        with dve.If(extra_b > 1):
                            for t in range(1, EXTRA):
                                if t > 1:
                                    steps(t - 1, t - 1)
                                with dve.If(extra_b > EXTRA - t):
                                    extra(t)
                        with dve.Else():
                            steps(1, EXTRA - 2)
                        with dve.If(extra_b > 0):
                            extra(EXTRA)
                        steps(EXTRA - 1, STATIC - 1)
                        with dve.If(extra_a > 0):
                            extra(STATIC + 1)
                        steps(STATIC, STATIC)
                        with dve.If(extra_a > 1):
                            for t in range(STATIC + 2, PAIR + 1):
                                with dve.If(extra_a > t - STATIC - 1):
                                    extra(t)
                                steps(t - 1, t - 1)
                        with dve.Else():
                            steps(STATIC + 1, PAIR - 1)
                        steps(PAIR, PAIR)
                        tail(dve, "dve", b, par, pair, word, done, tail_slot)
                    with dve.Else():
                        steps(1, PAIR)
                dve.wait_ge(max_done, SLOTS * (b + 1))
                dve.sem_inc(agg_done, 1)

            for k in range(K):
                stats_of(0, k)
            for k in range(K):
                means_of(0, k)
            def codes_first(k):
                for half in range(H):
                    dve.wait_ge(number_ready, H * k + half + 1)
                    dve.tensor_scalar(code[:, 0, k, half * WIDTH:(half + 1) * WIDTH], number_first(half), 0.5,
                                      code_bias[:, :], ALU.mult, ALU.add).then_inc(code_ready, 1)

            AHEAD = 3
            for k in range(K + AHEAD):
                if k < K:
                    dve.wait_ge(adj_loaded[k], 16)
                    dve.tensor_scalar(nonedge[:, k, :], adj_in[:, k, :], 0.0, None, ALU.is_equal).then_inc(nonedge_ready, 1)
                if k == AHEAD:
                    dve.wait_ge(bias_ready, 3)
                if k >= AHEAD:
                    codes_first(k - AHEAD)
            dve.wait_ge(w_loaded, 48)
            dve.tensor_scalar(w_sb[:, :, :], w_in[:, :, :], 1.0 / SCALE, None, ALU.mult).then_inc(w_ready, 1)
            for n in range(LOOKAHEAD):
                make_onehots(0, 0, n)
            done = dve.alloc_register("tail_slots_done")
            extras = dve.alloc_register("extras_made")
            dve.reg_mov(done, 0)
            dve.reg_mov(extras, 0)
            body(0, 0, 1, False, done, extras)
            with dve.Fori(1, B - 1) as b:
                body(b, b & 1, (b + 1) & 1, False, done, extras)
            body(B - 1, (B - 1) & 1, 0, True, done, extras)
            dve.wait_ge(xT_loaded, 16 * B)
            dve.wait_ge(stored, 16 * (B - 1))
            for half in range(H):
                cols = slice(half * WIDTH, (half + 1) * WIDTH)
                dve.wait_ge(dense_read, 4 * B + half)
                dve.tensor_tensor(out_sb[:, cols], act_out[:, cols], xT_in[:, cols], ALU.add).then_inc(last_added, 1)

        @block.tensor
        def _(pe):
            pe.wait_ge(const_ready, 4 + 2 * K)

            def order(nb, p):
                half, k = divmod(p, K)
                cols = slice(half * WIDTH, (half + 1) * WIDTH)
                pe.wait_ge(nonedge_ready, K * nb + k + 1)
                if not (isinstance(nb, int) and nb == 0 and p == 0):
                    pe.wait_ge(valid_ready, PREP * nb + p)
                if k:
                    pe.matmul(ordinal_ps[:, :], count_rest[:, :], nonedge[:, k - 1, cols], start=False, stop=False,
                              skip_group_check=True)
                pe.matmul(ordinal_ps[:, :], count_here[:, :], nonedge[:, k, cols], start=(k == 0), stop=True,
                          skip_group_check=True).then_inc(ordinal_ready, 1)

            def renumber(nb, p):
                half, k = divmod(p, K)
                pe.wait_ge(valid_ready, PREP * nb + p + 1)
                if not (isinstance(nb, int) and nb == 0 and p == 0):
                    pe.wait_ge(code_ready, PREP * nb + p)
                if k == 0 and not (isinstance(nb, int) and nb == 0 and half == 0):
                    pe.wait_ge(over_ready, H * nb + half)
                pe.matmul(degree_ps[:, :], pick_row[:, k, :], valid[:, p % VALIDS, :], start=(k == 0), stop=(k == K - 1),
                          skip_group_check=True)
                pe.matmul(number_ps[:, :], number[:, :], valid[:, p % VALIDS, :], start=True,
                          stop=True).then_inc(number_ready, 1)

            def products(buf, par, k, hot, start, stop):
                for part in range(2):
                    for half in range(H):
                        cols = slice(half * WIDTH, (half + 1) * WIDTH)
                        last = pe.matmul(buf[:, cols], h16[:, par, part, k, :], hot[:, cols],
                                         start=(start and part == 0), stop=(stop and part == 1))
                return last

            def hot_of(b, pair, t, q):
                if t in FROM_ACT:
                    j = pair * BY_ACT + FROM_ACT.index(t)
                    pe.wait_ge(act_onehot_ready, PAIRS * BY_ACT * b + j + 2)
                    return act_onehot[:, j % BY_ACT, :]
                i = onehot_index(pair, t, q)
                pe.wait_ge(onehot_ready, PAIRS * len(BY_DVE) * b + i + 1)
                return onehot[:, i % ONEHOTS, :]

            def gather(b, par, n, clash=False, extras=None):
                pair, t = n // PAIR, n % PAIR + 1
                if n > 1 or not (isinstance(b, int) and b == 0):
                    pe.wait_ge(max_done, SLOTS * b + n - 1)
                taken = parts(t)[:1] if clash else parts(t)
                for q, (c, s) in enumerate(taken):
                    last = products(gathered[n % 2], par, 2 * pair + c, hot_of(b, pair, t, q), q == 0,
                                    q == len(taken) - 1 and extras is None)
                if extras is not None:
                    pe.reg_add(extras, extras, 1)
                    pe.wait_ge(extra_ready, pe.snap(extras))
                    last = products(gathered[n % 2], par, 2 * pair + (1 if t <= EXTRA else 0), extra_onehot[:, t % 2, :],
                                    False, True)
                last.then_inc(gather_ready, 1)

            def tail_slot(b, par, k, n_next, s, done):
                pe.reg_add(done, done, 1)
                d = pe.snap(done)
                pe.wait_ge(max_done, SLOTS * b + n_next - 1)
                pe.wait_ge(tail_onehot_ready, d)
                products(gathered[n_next % 2], par, k, tail_onehot, True, True).then_inc(tail_gather_ready, 1)
                hold(pe, "pe", tail_max_done, d)

            def transpose_h(b, par, half):
                pe.wait_ge(dense_read, 4 * b + half + 1)
                chunks = WIDTH // P
                for q in range(chunks):
                    for part in range(2):
                        last = pe.matmul(dense_ps[:, q * P:(q + 1) * P], h16[:, par, part, half * chunks + q, :],
                                         ident[:, :], start=(part == 0), stop=(part == 1))
                last.then_inc(dense_ready, 1)

            def dense(b, par, half):
                cols = slice(half * WIDTH, (half + 1) * WIDTH)
                if half == 0:
                    pe.wait_ge(agg_done, b + 1)
                pe.wait_ge(dense_read, 4 * b + 3 + half)
                pe.matmul(dense_ps[:, :], w_sb[:, 0, :], hT[:, cols], start=True, stop=False)
                pe.matmul(dense_ps[:, :], w_sb[:, 1, :], agg[:, par, cols], start=False, stop=True).then_inc(dense_ready, 1)

            def body(b, par, par_next, first, last, done, extras):
                pe.wait_ge(lo_ready, b + 1)

                def step(n, **how):
                    gather(b, par, n, **how)
                    if not last and n in ORDER_AT:
                        order(b + 1, ORDER_AT[n])
                    if not last and n in RENUMBER_AT:
                        renumber(b + 1, RENUMBER_AT[n])
                    if not first and n in DENSE_AT:
                        dense(b - 1, 1 - par, DENSE_AT[n])
                    if n in TRANSPOSE_AT:
                        transpose_h(b, par, TRANSPOSE_AT[n])

                flags = flags_of(pe, "pe", b, par)
                for pair in range(PAIRS):
                    def steps(first_t, last_t, **how):
                        for t in range(first_t, last_t + 1):
                            step(PAIR * pair + t - 1, **how)

                    def step_if(condition, t):
                        with pe.If(condition):
                            steps(t, t, extras=extras)
                        with pe.Else():
                            steps(t, t)

                    with pe.If((flags >> pair) & 1 > 0):
                        word = Word(pe, par, pair)
                        extra_a, extra_b = word.extra
                        with pe.If(extra_b > 1):
                            for t in range(1, EXTRA):
                                step_if(extra_b > EXTRA - t, t)
                        with pe.Else():
                            steps(1, EXTRA - 1)
                        step_if(extra_b > 0, EXTRA)
                        with pe.If(word.clash > 0):
                            steps(EXTRA + 1, STATIC, clash=True)
                        with pe.Else():
                            steps(EXTRA + 1, STATIC)
                        step_if(extra_a > 0, STATIC + 1)
                        with pe.If(extra_a > 1):
                            for t in range(STATIC + 2, PAIR + 1):
                                step_if(extra_a > t - STATIC - 1, t)
                        with pe.Else():
                            steps(STATIC + 2, PAIR)
                        tail(pe, "pe", b, par, pair, word, done, tail_slot)
                    with pe.Else():
                        steps(1, PAIR)

            def order_first(p):
                k, half = divmod(p, H)
                cols = slice(half * WIDTH, (half + 1) * WIDTH)
                pe.wait_ge(nonedge_ready, k + 1)
                if k:
                    pe.wait_ge(valid_ready, p - H + 1)
                    pe.matmul(ordinal_first(half), count_rest[:, :], nonedge[:, k - 1, cols], start=False, stop=False,
                              skip_group_check=True)
                pe.matmul(ordinal_first(half), count_here[:, :], nonedge[:, k, cols], start=(k == 0), stop=True,
                          skip_group_check=True).then_inc(ordinal_ready, 1)

            def renumber_first(p):
                k, half = divmod(p, H)
                pe.wait_ge(valid_ready, p + 1)
                if k:
                    pe.wait_ge(code_ready, p - H + 1)
                pe.matmul(degree_first(half), pick_row[:, k, 0:K + PAIRS], valid[:, p % VALIDS, :], start=(k == 0),
                          stop=(k == K - 1), skip_group_check=True)
                pe.matmul(number_first(half), number[:, :], valid[:, p % VALIDS, :], start=True,
                          stop=True).then_inc(number_ready, 1)

            for p in range(H):
                order_first(p)
            for p in range(PREP):
                if p + H < PREP:
                    order_first(p + H)
                renumber_first(p)
            pe.wait_ge(code_ready, PREP)
            pe.wait_ge(over_ready, H)
            pe.wait_ge(w_ready, 1)
            done = pe.alloc_register("tail_slots_done")
            extras = pe.alloc_register("extras_taken")
            pe.reg_mov(done, 0)
            pe.reg_mov(extras, 0)
            body(0, 0, 1, True, False, done, extras)
            with pe.Fori(1, B - 1) as b:
                body(b, b & 1, (b + 1) & 1, False, False, done, extras)
            body(B - 1, (B - 1) & 1, 0, False, True, done, extras)
            for half in range(H):
                dense(B - 1, (B - 1) & 1, half)


def kernel(x, adj, L0_gnn_W, L0_gnn_b):
    import numpy as np
    import concourse.bacc as bacc
    from concourse.bass_utils import run_bass_kernel_spmd

    x = np.asarray(x)
    arrays = {
        "x": np.ascontiguousarray(x),
        "x_by_channel": np.ascontiguousarray(x.transpose(0, 2, 1)),
        "adj_by_source": np.ascontiguousarray(np.asarray(adj).transpose(0, 2, 1)),
        "W": np.ascontiguousarray(L0_gnn_W),
        "b": np.ascontiguousarray(L0_gnn_b),
    }
    nc = bacc.Bacc("TRN2", target_bir_lowering=False, num_devices=1)
    args = [nc.dram_tensor(name, a.shape, mybir.dt.from_np(a.dtype), kind="ExternalInput").ap()
            for name, a in arrays.items()]
    B, N, C = x.shape
    out = nc.dram_tensor("out_by_channel", (B, C, N), F32, kind="ExternalOutput").ap()
    adj_preln_kernel(nc, *args, out)
    r = run_bass_kernel_spmd(nc, [arrays], core_ids=[0])
    return np.ascontiguousarray(r.results[0]["out_by_channel"].transpose(0, 2, 1))
```
